# Optimizing a Trainium2 kernel written in Bass

```python
import numpy as np
import jax
import jax.numpy as jnp

def _softmax(x, axis=-1):
    return jax.nn.softmax(x, axis=axis)

def _gelu(x):
    return jax.nn.gelu(x, approximate=True)

def _silu(x):
    return jax.nn.silu(x)

def _sigmoid(x):
    return jax.nn.sigmoid(x)

def _layernorm(x, axis=-1, eps=1e-05):
    m = jnp.mean(x, axis=axis, keepdims=True)
    v = jnp.var(x, axis=axis, keepdims=True)
    return (x - m) / jnp.sqrt(v + eps)

def _scatter_add(tgt, idx, src, axis=0):
    return tgt.at[idx].add(src)

def _segment_sum(src, seg, n):
    return jax.ops.segment_sum(src, seg, n)
kernel_name = 'mk_xattn_seq_d2_seqx_r2_f9e0b3'

def setup_inputs(seed: int=0):
    np.random.seed(seed)
    _w = jnp.asarray

    def _rec_inputs():
        import jax
        import jax.numpy as jnp
        _rk = jax.random.key(seed)
        x = -0.0003929 + 0.9999 * jax.random.normal(jax.random.fold_in(_rk, 1), (64, 256, 512), jnp.float32)
        _lenS = 256 - jax.random.randint(jax.random.fold_in(_rk, 7), (64,), 0, max(1, 256 // 4) + 1, jnp.int32)
        _lenS2 = 256 - jax.random.randint(jax.random.fold_in(_rk, 8), (64,), 0, max(1, 256 // 4) + 1, jnp.int32)
        _ctx_512P = jax.random.normal(jax.random.fold_in(_rk, 11), (64, 16, 256), jnp.float32)
        _ctx_512c = jax.random.dirichlet(jax.random.fold_in(_rk, 511), 0.3 * jnp.ones((16,), jnp.float32), (64, 256))
        _ctx_512t = jnp.einsum('bsk,bkd->bsd', _ctx_512c, _ctx_512P)
        _ctx_512t = _ctx_512t * jax.lax.rsqrt(jnp.mean(jnp.square(_ctx_512t)) + 1e-12) * 0.953939
        ctx_512 = 4.13588e-05 + 0.999923 * (_ctx_512t + 0.3 * jax.random.normal(jax.random.fold_in(_rk, 611), (64, 256, 256), jnp.float32))
        return (x, ctx_512)
    x, ctx_512 = _rec_inputs()

    def _L0_xattn_setup():
        import jax, jax.numpy as jnp
        import numpy as np
        QUERY_DIM = 512
        KEY_DIM = 256
        HIDDEN_DIM = 512
        B, LQ, LK = (8, 1024, 1024)
        key = jax.random.key(seed)
        ks = jax.random.split(key, 10)
        s_q = 1.0 / np.sqrt(QUERY_DIM)
        s_k = 1.0 / np.sqrt(KEY_DIM)
        s_h = 1.0 / np.sqrt(HIDDEN_DIM)
        return {'query': jax.random.normal(ks[0], (B, LQ, QUERY_DIM), jnp.float32), 'key': jax.random.normal(ks[1], (B, LK, KEY_DIM), jnp.float32), 'Wq': jax.random.uniform(ks[2], (QUERY_DIM, HIDDEN_DIM), jnp.float32, -s_q, s_q), 'bq': jax.random.uniform(ks[3], (HIDDEN_DIM,), jnp.float32, -s_q, s_q), 'Wk': jax.random.uniform(ks[4], (KEY_DIM, HIDDEN_DIM), jnp.float32, -s_k, s_k), 'bk': jax.random.uniform(ks[5], (HIDDEN_DIM,), jnp.float32, -s_k, s_k), 'Wv': jax.random.uniform(ks[6], (KEY_DIM, HIDDEN_DIM), jnp.float32, -s_k, s_k), 'bv': jax.random.uniform(ks[7], (HIDDEN_DIM,), jnp.float32, -s_k, s_k), 'Wo': jax.random.uniform(ks[8], (HIDDEN_DIM, QUERY_DIM), jnp.float32, -s_h, s_h), 'bo': jax.random.uniform(ks[9], (QUERY_DIM,), jnp.float32, -s_h, s_h)}
    _L0_xattn_all = _L0_xattn_setup()
    _L0_xattn_in = {k: v for k, v in _L0_xattn_all.items() if k in ('Wq', 'bq', 'Wk', 'bk', 'Wv', 'bv', 'Wo', 'bo')}
    del _L0_xattn_all

    def _L1_xattn_setup():
        import jax, jax.numpy as jnp
        import numpy as np
        B, T, E = (8, 2048, 512)
        M, L = (128, 256)
        EPS = 1e-06
        key = jax.random.key(seed)
        ks = jax.random.split(key, 5)
        return {'emb': jax.random.normal(ks[0], (B, T, E), dtype=jnp.float32), 'latent': jax.random.normal(ks[1], (B, M, L), dtype=jnp.float32), 'Wq': jax.random.normal(ks[2], (E, E), dtype=jnp.float32) * (1.0 / np.sqrt(E)), 'bq': jnp.zeros((E,), dtype=jnp.float32), 'Wk': jax.random.normal(ks[3], (L, E), dtype=jnp.float32) * (1.0 / np.sqrt(L)), 'bk': jnp.zeros((E,), dtype=jnp.float32), 'Wv': jax.random.normal(ks[4], (L, E), dtype=jnp.float32) * (1.0 / np.sqrt(L)), 'bv': jnp.zeros((E,), dtype=jnp.float32), 'gamma': jnp.ones((E,), dtype=jnp.float32), 'beta': jnp.zeros((E,), dtype=jnp.float32)}
    _L1_xattn_all = _L1_xattn_setup()
    _L1_xattn_in = {k: v for k, v in _L1_xattn_all.items() if k in ('Wq', 'bq', 'Wk', 'bk', 'Wv', 'bv', 'gamma', 'beta')}
    del _L1_xattn_all
    return {'x': x, 'ctx_512': ctx_512, 'L0_xattn_Wq': _L0_xattn_in['Wq'], 'L0_xattn_bq': _L0_xattn_in['bq'], 'L0_xattn_Wk': _L0_xattn_in['Wk'], 'L0_xattn_bk': _L0_xattn_in['bk'], 'L0_xattn_Wv': _L0_xattn_in['Wv'], 'L0_xattn_bv': _L0_xattn_in['bv'], 'L0_xattn_Wo': _L0_xattn_in['Wo'], 'L0_xattn_bo': _L0_xattn_in['bo'], 'L1_xattn_Wq': _L1_xattn_in['Wq'], 'L1_xattn_bq': _L1_xattn_in['bq'], 'L1_xattn_Wk': _L1_xattn_in['Wk'], 'L1_xattn_bk': _L1_xattn_in['bk'], 'L1_xattn_Wv': _L1_xattn_in['Wv'], 'L1_xattn_bv': _L1_xattn_in['bv'], 'L1_xattn_gamma': _L1_xattn_in['gamma'], 'L1_xattn_beta': _L1_xattn_in['beta']}

def reference(x, ctx_512, L0_xattn_Wq, L0_xattn_bq, L0_xattn_Wk, L0_xattn_bk, L0_xattn_Wv, L0_xattn_bv, L0_xattn_Wo, L0_xattn_bo, L1_xattn_Wq, L1_xattn_bq, L1_xattn_Wk, L1_xattn_bk, L1_xattn_Wv, L1_xattn_bv, L1_xattn_gamma, L1_xattn_beta):
    import jax
    import jax.numpy as jnp

    def _L0_xattn_ref(query, key, Wq, bq, Wk, bk, Wv, bv, Wo, bo):
        import jax, jax.numpy as jnp
        import numpy as np
        QUERY_DIM = 512
        KEY_DIM = 256
        HIDDEN_DIM = 512
        B, LQ, LK = (8, 1024, 1024)
        scale = HIDDEN_DIM ** (-0.5)
        Q = jnp.einsum('bqd,dh->bqh', query, Wq) + bq
        K = jnp.einsum('bkd,dh->bkh', key, Wk) + bk
        V = jnp.einsum('bkd,dh->bkh', key, Wv) + bv
        scores = jnp.einsum('bqh,bkh->bqk', Q, K) * scale
        weights = jax.nn.softmax(scores, axis=-1)
        attended = jnp.einsum('bqk,bkh->bqh', weights, V)
        out = jnp.einsum('bqh,hd->bqd', attended, Wo) + bo
        return query + out

    def _L1_xattn_ref(emb, latent, Wq, bq, Wk, bk, Wv, bv, gamma, beta):
        import jax, jax.numpy as jnp
        import numpy as np
        B, T, E = (8, 2048, 512)
        M, L = (128, 256)
        EPS = 1e-06
        q = jnp.einsum('bte,ef->btf', emb, Wq) + bq
        k = jnp.einsum('bml,le->bme', latent, Wk) + bk
        v = jnp.einsum('bml,le->bme', latent, Wv) + bv
        scale = 1.0 / jnp.sqrt(jnp.asarray(E, dtype=q.dtype))
        w = jnp.einsum('bte,bme->btm', q, k) * scale
        w = jax.nn.softmax(w, axis=1)
        pred = jnp.einsum('btm,bme->bte', w, v)
        x = pred + emb
        mu = jnp.mean(x, axis=-1, keepdims=True)
        var = jnp.var(x, axis=-1, keepdims=True)
        return (x - mu) * jax.lax.rsqrt(var + EPS) * gamma + beta
    x = _L0_xattn_ref(x, ctx_512, L0_xattn_Wq, L0_xattn_bq, L0_xattn_Wk, L0_xattn_bk, L0_xattn_Wv, L0_xattn_bv, L0_xattn_Wo, L0_xattn_bo)
    x = _L1_xattn_ref(x, ctx_512, L1_xattn_Wq, L1_xattn_bq, L1_xattn_Wk, L1_xattn_bk, L1_xattn_Wv, L1_xattn_bv, L1_xattn_gamma, L1_xattn_beta)
    return x

_drawn_inputs = setup_inputs


def setup_inputs(seed=0):
    import zlib

    import numpy as np

    out = dict(_drawn_inputs(seed))
    spreads = {'L1_xattn_bq': (0.0, 0.8),
     'L1_xattn_bk': (0.0, 0.1),
     'L1_xattn_bv': (0.0, 0.1),
     'L1_xattn_gamma': (1.0, 0.2),
     'L1_xattn_beta': (0.0, 0.1)}
    factors = {'L0_xattn_Wq': 3.03,
     'L0_xattn_bq': 8.0,
     'L0_xattn_Wk': 3.017,
     'L0_xattn_bk': 8.0,
     'L0_xattn_bv': 3.262}
    for name, (base, spread) in spreads.items():
        noise = np.random.default_rng([zlib.crc32(name.encode()), seed]).standard_normal(out[name].shape)
        drawn = base * np.exp(spread * noise) if base else spread * noise
        out[name] = jnp.asarray(drawn.astype(out[name].dtype))
    for name, factor in factors.items():
        out[name] = (out[name] * factor).astype(out[name].dtype)
    return out
```

```python
import concourse.bass as bass
from concourse import mybir
from contextlib import ExitStack

P = 128
NSEQ, S, D, L = 64, 256, 512, 256
H = 512
PAIRS = NSEQ // 2
DT, LT, HT, ST = D // P, L // P, H // P, S // P
W = 2 * S
SCALE = float(H) ** -0.5
EPS = 1e-6

TP_BODY = ["PTa", "PTb", "cT0", "cT1", "xT0", "xT1", "xT2", "xT3", "yTa0", "yTa1", "yTb0", "yTb1"]
PJ_BODY = ["G2", "G3", "Pa", "Pb", "u0", "u1", "wa", "G0", "wb", "G1"]
SC_BODY = ["S1a", "S1b", "S0a", "S0b", "sa", "sb"]
OT_BODY = ["out0", "out1", "out2", "out3", "pred0", "pred1", "pred2", "pred3"]
TP_FRONT = ["cT0", "cT1", "xT0", "xT1", "xT2", "xT3"]
PJ_FRONT = ["u0", "u1", "G0", "G1"]
SC_FRONT = ["S0a", "S0b"]


class Ring:

    def __init__(self, front, body):
        self.front, self.body = front, body
        self.last = [n for n in body if n not in front or n in ("G2", "G3")]

    def index(self, name, i, last):
        if i is None:
            return self.front.index(name)
        return (self.last if last else self.body).index(name)

    def number(self, name, i, last=False):
        if i is None:
            return self.index(name, i, last)
        return i * len(self.body) + (len(self.front) + self.index(name, i, last))

    def bank(self, name, i, last=False):
        return self.index(name, i, last) % 2


TP, PJ, SC, OT = (Ring(TP_FRONT, TP_BODY), Ring(PJ_FRONT, PJ_BODY), Ring(SC_FRONT, SC_BODY),
                  Ring([], OT_BODY))


def build(nc, x, ctxt, Wq0, bq0, Wk0, Wv0, bv0, Wo0, bo0, Wq1, Wk1, bk1, Wv1, bv1, gamma, beta, out):
    f32, f32r = mybir.dt.float32, mybir.dt.float32r
    ALU, ACT, AX = mybir.AluOpType, mybir.ActivationFunctionType, mybir.AxisListType

    x_v = x.rearrange("(n s) (p q) d -> n p s (q d)", s=2, q=ST)
    c_v = ctxt.rearrange("(n s) (p q) d -> n p s (q d)", s=2, q=ST)
    o_v = out.rearrange("(n s) (p q) d -> n p s (q d)", s=2, q=ST)

    with ExitStack() as stack:
        def sb(name, shape, dt=f32):
            return stack.enter_context(nc.sbuf_tensor(name, shape, dt))

        def split(name, shape):
            return [sb(name + "_hi", shape, f32r), sb(name + "_lo", shape, f32r)]

        def sem(name):
            return stack.enter_context(nc.semaphore(name))

        ident = sb("ident", [P, P])
        A0 = split("A0", [P, DT, L])
        Bv = split("Bv", [P, LT, D])
        A1T = split("A1T", [P, LT, D])
        V1 = split("V1", [P, LT, D])
        ones = sb("ones", [P, 2], f32r)
        ones_f = sb("ones_f", [P, P])
        c0 = sb("c0", [P, LT])
        g1 = sb("g1", [P, DT])
        c1_b = sb("c1_b", [P, D])
        bv1_b = sb("bv1_b", [P, D])
        gamma_b = sb("gamma_b", [P, D])
        beta_b = sb("beta_b", [P, D])
        bcol = sb("bcol", [P, 3, HT])
        half = sb("half", [P, 2 * ST])

        X = sb("X", [P, 2 * ST, D])
        R = [sb(f"R{n}", [P, 2 * ST, D]) for n in range(2)]
        Y = sb("Y", [P, 2 * ST, D])
        C = sb("C", [P, 2 * ST, L])
        Cs = [split(f"C{n}", [P, 2 * ST, L]) for n in range(2)]
        cT = split("cT", [P, LT, W])
        xT = split("xT", [P, DT, W])
        uT = split("uT", [P, LT, W])
        G = split("G", [P, DT, W])
        E0 = sb("E0", [P, 2 * ST, S])
        PT = split("PT", [P, 2, ST, S])
        PcT = split("PcT", [P, 2, LT, S])
        yT = split("yT", [P, 2, DT, S])
        E1 = sb("E1", [P, 2 * ST, S])
        w = split("w", [P, 2, ST, S])
        wcT = split("wcT", [P, 2, LT, S])
        sbv = sb("sbv", [P, 2, D])
        nmax0, Z0, rz0 = sb("nmax0", [P, 4]), sb("Z0", [P, 4]), sb("rz0", [P, 4])
        nmax1, Z1, rz1 = sb("nmax1", [P, 4]), sb("Z1", [P, 4]), sb("rz1", [P, 4])
        s_sb = sb("s_sb", [P, 4])
        stats = sb("stats", [P, 4, 6])
        msum = sb("msum", [P, 4, 2])
        mdif, msq, vin = (sb(n, [P, 4]) for n in ("mdif", "msq", "vin"))
        ve, rstd, nmu, nmr = (sb(n, [P, 4]) for n in ("ve", "rstd", "nmu", "nmr"))

        bank = [stack.enter_context(nc.psum_tensor(f"bank{n}", [P, 512], f32)) for n in range(8)]
        tp_bank, pj_bank, sc_bank, ot_bank = bank[0:2], bank[2:4], bank[4:6], bank[6:8]

        w_in = [sem(f"w_in{n}") for n in range(7)]
        b_in = sem("b_in")
        const_set = sem("const_set")
        su_full = sem("su_full")
        su_act, su_dve = sem("su_act"), sem("su_dve")
        x_in, c_in, y_out = sem("x_in"), sem("c_in"), sem("y_out")
        tp_full, tp_hi, tp_free = sem("tp_full"), sem("tp_hi"), sem("tp_free")
        pj_full, pj_hi, pj_free = sem("pj_full"), sem("pj_hi"), sem("pj_free")
        sc_full, sc_free = sem("sc_full"), sem("sc_free")
        ot_full, ot_free = sem("ot_full"), sem("ot_free")
        neg_max = sem("neg_max")
        rz1_set = sem("rz1_set")
        w_hi, w_lo = sem("w_hi"), sem("w_lo")
        Cs_set = sem("Cs_set")
        R_set = sem("R_set")
        sbv_set = sem("sbv_set")
        R_sbv = sem("R_sbv")
        mv_set = sem("mv_set")
        norm_set = sem("norm_set")
        Y_set = sem("Y_set")
        Y_mul = sem("Y_mul")
        Y_done = sem("Y_done")
        Cs_hi = sem("Cs_hi")
        norm_step = sem("norm_step")
        dve_step = sem("dve_step")

        XS = X[:, :, :].rearrange("p a b -> p (a b)")
        WqN = R[0][:, :, :]
        WqT = R[1][:, :, :]
        WkN = E0[:, :, :].rearrange("p a b -> p (a b)").rearrange("p (t n) -> p t n", t=LT)
        WkT = E1[:, :, :]
        WvN = sbv[:, :, :]
        WvT = XS[:, 0:HT * L].rearrange("p (t n) -> p t n", t=HT)
        WoN = Y[:, :, :]
        bvw = XS[:, HT * L:HT * L + HT * P].rearrange("p (t n) -> p t n", t=HT)

        block = stack.enter_context(nc.Block())

        def fp(ap):
            return ap.bitcast(f32)

        @block.sync
        def _(sp):
            def rows(a):
                return a.rearrange("(t p) n -> p t n", p=P)

            sp.dma_start(WqN, rows(Wq0)).then_inc(w_in[0], 16)
            sp.dma_start(WkN, rows(Wk0)).then_inc(w_in[1], 16)
            sp.dma_start(WvN, rows(Wv0)).then_inc(w_in[2], 16)
            sp.dma_start(WoN, Wo0.rearrange("(p t) n -> p t n", p=P)).then_inc(w_in[3], 16)
            sp.dma_start(C[:, :, :].rearrange("p (s q) l -> p s (q l)", s=2), c_v[0]).then_inc(c_in, 16)
            sp.wait_ge(su_full, 6)
            sp.dma_start(WqN, rows(Wq1)).then_inc(w_in[4], 16)
            sp.dma_start(WkN, rows(Wk1)).then_inc(w_in[5], 16)
            sp.wait_ge(su_full, 8)
            sp.dma_start(WvN, rows(Wv1)).then_inc(w_in[6], 16)
            sp.wait_ge(su_full, 13)
            sp.dma_start(X[:, :, :].rearrange("p (s q) d -> p s (q d)", s=2), x_v[0]).then_inc(x_in, 16)

            def load(n):
                first = isinstance(n, int) and n == 1
                sp.wait_ge(tp_full, TP.number("cT1", None if first else n - 2) + 1)
                sp.wait_ge(Cs_set, n)
                sp.dma_start(C[:, :, :].rearrange("p (s q) l -> p s (q l)", s=2), c_v[n]).then_inc(c_in, 16)
                sp.wait_ge(R_set, n)
                sp.dma_start(X[:, :, :].rearrange("p (s q) d -> p s (q d)", s=2), x_v[n]).then_inc(x_in, 16)

            def store(i):
                sp.wait_ge(Y_done, i + 1)
                sp.dma_start(o_v[i], Y[:, :, :].rearrange("p (s q) d -> p s (q d)", s=2)).then_inc(y_out, 16)

            load(1)
            with sp.Fori(2, PAIRS) as n:
                load(n)
                store(n - 2)
            store(PAIRS - 2)
            store(PAIRS - 1)
            sp.wait_ge(y_out, 16 * PAIRS)

        @block.tensor
        def _(pe):
            def product(dst, stat, mov, k):
                for t in range(k):
                    for n, (a, b) in enumerate(((0, 0), (0, 1), (1, 0))):
                        last = nc.tensor.matmul(dst, stat(a, t), mov(b, t), start=(t == 0 and n == 0),
                                                stop=(t == k - 1 and n == 2))
                return last

            def transposes(dst, src):
                for n, s in enumerate(src):
                    last = nc.tensor.transpose(dst[:, n * P:(n + 1) * P], s, ident[:, :])
                return last

            pe.wait_ge(const_set, 2)
            pe.wait_ge(w_in[0], 16)
            for h in range(HT):
                transposes(bank[h], [WqN[:, d, h::HT] for d in range(DT)]).then_inc(su_full, 1)
            pe.wait_ge(w_in[1], 16)
            for h in range(0, HT, 2):
                transposes(bank[4 + h // 2], [WkN[:, l, k::HT] for k in (h, h + 1)
                                              for l in range(LT)]).then_inc(su_full, 1)
            pe.wait_ge(w_in[2], 16)
            for h in range(0, HT, 2):
                transposes(bank[6 + h // 2], [WvN[:, l, k::HT] for k in (h, h + 1)
                                              for l in range(LT)]).then_inc(su_full, 1)
            pe.wait_ge(su_act, 4)
            pe.wait_ge(su_dve, 3)
            for d in range(0, DT, 2):
                for k in (d, d + 1):
                    for h in range(HT):
                        last = nc.tensor.matmul(bank[d // 2][:, (k - d) * L:(k - d + 1) * L],
                                                WqT[:, h, k * P:(k + 1) * P], WkT[:, h, :],
                                                start=(h == 0), stop=(h == HT - 1))
                last.then_inc(su_full, 1)
            pe.wait_ge(b_in, 7 * 16)
            for l in range(LT):
                for h in range(HT):
                    last = nc.tensor.matmul(bank[2][:, l:l + 1], WkT[:, h, l * P:(l + 1) * P],
                                            bcol[:, 0, h:h + 1], start=(h == 0), stop=(h == HT - 1))
            last.then_inc(su_full, 1)
            pe.wait_ge(su_dve, 5)
            pe.wait_ge(w_in[3], 16)
            for l in range(LT):
                for h in range(HT):
                    last = nc.tensor.matmul(bank[4 + l][:, :], WvT[:, h, l * P:(l + 1) * P], WoN[:, h, :],
                                            start=(h == 0), stop=(h == HT - 1))
            last.then_inc(su_full, 1)
            for h in range(HT):
                last = nc.tensor.matmul(bank[3][:, :], bvw[:, h, :], WoN[:, h, :],
                                        start=(h == 0), stop=(h == HT - 1))
            last.then_inc(su_full, 1)
            pe.wait_ge(su_dve, 10)
            pe.wait_ge(w_in[4], 16)
            for h in range(HT):
                transposes(bank[h], [WqN[:, d, h::HT] for d in range(DT)]).then_inc(su_full, 1)
            pe.wait_ge(w_in[5], 16)
            for h in range(0, HT, 2):
                transposes(bank[4 + h // 2], [WkN[:, l, k::HT] for k in (h, h + 1)
                                              for l in range(LT)]).then_inc(su_full, 1)
            pe.wait_ge(su_act, 11)
            pe.wait_ge(su_dve, 12)
            for l in range(LT):
                for h in range(HT):
                    last = nc.tensor.matmul(bank[6 + l][:, :], WkT[:, h, l * P:(l + 1) * P], WqT[:, h, :],
                                            start=(h == 0), stop=(h == HT - 1))
            last.then_inc(su_full, 1)
            for d in range(DT):
                for h in range(HT):
                    last = nc.tensor.matmul(bank[5][:, d:d + 1], WqT[:, h, d * P:(d + 1) * P],
                                            bcol[:, 2, h:h + 1], start=(h == 0), stop=(h == HT - 1))
            last.then_inc(su_full, 1)
            pe.wait_ge(su_dve, 16)

            def take(ring, name, i, last, free):
                k = ring.number(name, i, last)
                if not (isinstance(k, int) and k < 2):
                    pe.wait_ge(free, k - 1)

            def tp(name, i, last, src):
                take(TP, name, i, last, tp_free)
                transposes(tp_bank[TP.bank(name, i, last)], src).then_inc(tp_full, 1)

            def tp_ready(name, i, last):
                pe.wait_ge(tp_free, TP.number(name, i, last) + 1)

            def pj_ready(name, i, last):
                pe.wait_ge(pj_free, PJ.number(name, i, last) + 1)

            def cT_(l, i):
                tp(f"cT{l}", i, False, [C[:, r, l * P:(l + 1) * P] for r in range(4)])

            def xT_(d, i):
                tp(f"xT{d}", i, False, [X[:, r, d * P:(d + 1) * P] for r in range(4)])

            def u_(l, i):
                take(PJ, f"u{l}", i, False, pj_free)
                product(pj_bank[PJ.bank(f"u{l}", i)][:, :], lambda a, t: A0[a][:, t, l * P:(l + 1) * P],
                        lambda b, t: xT[b][:, t, :], DT).then_inc(pj_full, 1)

            def G_(d, i, last):
                take(PJ, f"G{d}", i, last, pj_free)
                product(pj_bank[PJ.bank(f"G{d}", i, last)][:, :],
                        lambda a, t: A1T[a][:, t, d * P:(d + 1) * P],
                        lambda b, t: cT[b][:, t, :], LT).then_inc(pj_full, 1)

            def S0_(s, i):
                name = "S0" + "ab"[s]
                take(SC, name, i, False, sc_free)
                for q in range(ST):
                    r = s * S + q * P
                    last = product(sc_bank[SC.bank(name, i)][:, q * S:(q + 1) * S],
                                   lambda a, t: uT[a][:, t, r:r + P],
                                   lambda b, t: cT[b][:, t, s * S:(s + 1) * S], LT)
                last.then_inc(sc_full, 1)

            def PT_(s, i, last):
                name = "PT" + "ab"[s]
                if isinstance(i, int) and i == 0:
                    pe.wait_ge(sc_free, SC.number("S0" + "ab"[s], None) + 1)
                else:
                    pe.wait_ge(sc_free, SC.number("S0" + "ab"[s], i - 1) + 1)
                tp(name, i, last, [E0[:, 2 * s + q, k * P:(k + 1) * P] for k in range(ST) for q in range(ST)])

            def Pc_(s, i, last, par):
                name = "P" + "ab"[s]
                tp_ready("PT" + "ab"[s], i, last)
                if s == 0:
                    pe.wait_ge(Cs_set, i + 1)
                take(PJ, name, i, last, pj_free)
                for l in range(LT):
                    done = product(pj_bank[PJ.bank(name, i, last)][:, l * S:(l + 1) * S],
                                   lambda a, t: Cs[par][a][:, 2 * s + t, l * P:(l + 1) * P],
                                   lambda b, t: PT[b][:, s, t, :], ST)
                done.then_inc(pj_full, 1)

            def out_(r, i, last):
                s, q = divmod(r, ST)
                if q == 0:
                    pj_ready("P" + "ab"[s], i, last)
                take(OT, f"out{r}", i, last, ot_free)
                product(ot_bank[OT.bank(f"out{r}", i)][:, :], lambda a, t: PcT[a][:, s, t, q * P:(q + 1) * P],
                        lambda b, t: Bv[b][:, t, :], LT).then_inc(ot_full, 1)

            def yT_(s, n, i, last):
                pe.wait_ge(ot_free, OT.number(f"out{2 * s + 1}", i, last) + 1)
                tp(f"yT{'ab'[s]}{n}", i, last, [R_(i, last)[:, 2 * s + q, d * P:(d + 1) * P]
                                                for d in (2 * n, 2 * n + 1) for q in range(ST)])

            def S1_(s, i, last):
                name = "S1" + "ab"[s]
                tp_ready(f"yT{'ab'[s]}1", i, last)
                take(SC, name, i, last, sc_free)
                if s == 0:
                    pj_ready("G3", i, last)
                for m in range(ST):
                    c = s * S + m * P
                    done = product(sc_bank[SC.bank(name, i, last)][:, m * S:(m + 1) * S],
                                   lambda a, t: G[a][:, t, c:c + P],
                                   lambda b, t: yT[b][:, s, t, :], DT)
                done.then_inc(sc_full, 1)

            def wc_(s, i, last, par):
                name = "w" + "ab"[s]
                pe.wait_ge(w_lo, 2 * i + (s + 1))
                take(PJ, name, i, last, pj_free)
                for l in range(LT):
                    done = product(pj_bank[PJ.bank(name, i, last)][:, l * S:(l + 1) * S],
                                   lambda a, t: Cs[par][a][:, 2 * s + t, l * P:(l + 1) * P],
                                   lambda b, t: w[b][:, s, t, :], ST)
                done.then_inc(pj_full, 1)

            def s_(s, i, last):
                name = "s" + "ab"[s]
                take(SC, name, i, last, sc_free)
                for q in range(ST):
                    for t in range(ST):
                        for a in range(2):
                            done = nc.tensor.matmul(sc_bank[SC.bank(name, i, last)][:, 2 * q:2 * q + 2],
                                                    w[a][:, s, t, q * P:(q + 1) * P], ones[:, :],
                                                    start=(t == 0 and a == 0), stop=(t == ST - 1 and a == 1))
                done.then_inc(sc_full, 1)

            def pred_(r, i, last):
                s, q = divmod(r, ST)
                if q == 0:
                    pj_ready("w" + "ab"[s], i, last)
                take(OT, f"pred{r}", i, last, ot_free)
                product(ot_bank[OT.bank(f"pred{r}", i)][:, :], lambda a, t: wcT[a][:, s, t, q * P:(q + 1) * P],
                        lambda b, t: V1[b][:, t, :], LT).then_inc(ot_full, 1)

            R_now = [None]

            def R_(i, last):
                return R_now[0]

            pe.wait_ge(c_in, 16)
            cT_(0, None)
            cT_(1, None)
            pe.wait_ge(x_in, 16)
            for d in range(DT):
                xT_(d, None)
            tp_ready("xT3", None, False)
            u_(0, None)
            u_(1, None)
            G_(0, None, False)
            G_(1, None, False)
            pj_ready("u1", None, False)
            S0_(0, None)
            S0_(1, None)

            def body(i, par, last):
                R_now[0] = R[par]
                PT_(0, i, last)
                G_(2, i, last)
                PT_(1, i, last)
                G_(3, i, last)
                Pc_(0, i, last, par)
                if not last:
                    pe.wait_ge(c_in, 16 * i + 32)
                    cT_(0, i)
                Pc_(1, i, last, par)
                if not last:
                    cT_(1, i)
                out_(0, i, last)
                if not last:
                    pe.wait_ge(x_in, 16 * i + 32)
                    xT_(0, i)
                out_(1, i, last)
                if not last:
                    xT_(1, i)
                out_(2, i, last)
                if not last:
                    xT_(2, i)
                out_(3, i, last)
                if not last:
                    xT_(3, i)
                yT_(0, 0, i, last)
                if not last:
                    tp_ready("xT3", i, last)
                    u_(0, i)
                yT_(0, 1, i, last)
                yT_(1, 0, i, last)
                if not last:
                    u_(1, i)
                yT_(1, 1, i, last)
                S1_(0, i, last)
                S1_(1, i, last)
                if not last:
                    pj_ready("u1", i, last)
                    S0_(0, i)
                    S0_(1, i)
                wc_(0, i, last, par)
                if not last:
                    G_(0, i, last)
                s_(0, i, last)
                wc_(1, i, last, par)
                if not last:
                    G_(1, i, last)
                s_(1, i, last)
                for r in range(4):
                    pred_(r, i, last)

            body(0, 0, False)
            body(1, 1, False)
            with pe.Fori(1, PAIRS // 2 - 1) as j:
                body(2 * j, 0, False)
                body(2 * j + 1, 1, False)
            body(PAIRS - 2, 0, False)
            body(PAIRS - 1, 1, True)

        @block.scalar
        def _(act):
            def copy(dst, src, **kw):
                return nc.scalar.activation(dst, src, ACT.Copy, **kw)

            for n, v in enumerate((bq0, bv0, bk1)):
                act.dma_start(bcol[:, n, :], v.rearrange("(p t) -> p t", p=P)).then_inc(b_in, 16)
            for dst, v in ((c1_b, bo0), (bv1_b, bv1), (gamma_b, gamma), (beta_b, beta)):
                act.dma_start(dst[:, :], v.rearrange("(a n) -> a n", a=1).to_broadcast([P, D])
                              ).then_inc(b_in, 16)
            for h in range(HT):
                act.wait_ge(su_full, h + 1)
                copy(WqT[:, h, :], bank[h][:, :]).then_inc(su_act, 1)
            act.wait_ge(su_full, 10)
            for n in range(2):
                copy(A0[0][:, 2 * n:2 * n + 2, :], bank[n][:, :].rearrange("p (a b) -> p a b", a=2),
                     scale=SCALE).then_inc(su_act, 1)
            act.wait_ge(su_full, 12)
            copy(Bv[0][:, 0, :], bank[4][:, :])
            copy(Bv[0][:, 1, :], bank[5][:, :]).then_inc(su_act, 1)
            for h in range(HT):
                act.wait_ge(su_full, 14 + h)
                copy(WqT[:, h, :], bank[h][:, :]).then_inc(su_act, 1)
            act.wait_ge(w_in[6], 16)
            copy(V1[0][:, :, :], WvN).then_inc(su_act, 1)
            act.wait_ge(su_full, 20)
            for l in range(LT):
                copy(A1T[0][:, l, :], bank[6 + l][:, :], scale=SCALE).then_inc(su_act, 1)

            def tp(name, i, last, dst):
                k = TP.number(name, i, last)
                act.wait_ge(tp_full, k + 1)
                copy(dst, tp_bank[TP.bank(name, i, last)][:, :]).then_inc(tp_hi, 1)

            def pj(name, i, last, dst, bias=None):
                k = PJ.number(name, i, last)
                act.wait_ge(pj_full, k + 1)
                src = pj_bank[PJ.bank(name, i, last)][:, :]
                if bias is None:
                    copy(dst, src).then_inc(pj_hi, 1)
                else:
                    nc.scalar.activation(dst, src, ACT.Identity, bias=bias).then_inc(pj_hi, 1)

            def exps(layer, s, i, last, count):
                name = f"S{layer}" + "ab"[s]
                E, Z, nmax = (E0, Z0, nmax0) if layer == 0 else (E1, Z1, nmax1)
                act.wait_ge(neg_max, count)
                for q in range(ST):
                    r = 2 * s + q
                    done = nc.scalar.activation(E[:, r, :],
                                                sc_bank[SC.bank(name, i, last)][:, q * S:(q + 1) * S],
                                                ACT.Exp, bias=nmax[:, r:r + 1], accum_out=Z[:, r:r + 1])
                done.then_inc(sc_free, 1)

            def w_(s, i):
                act.wait_ge(rz1_set, 2 * i + (s + 1))
                for m in range(ST):
                    r = 2 * s + m
                    done = copy(w[0][:, s, m, :], E1[:, r, :], scale=rz1[:, r:r + 1])
                done.then_inc(w_hi, 1)

            def s_(s, i, last):
                name = "s" + "ab"[s]
                act.wait_ge(sc_full, SC.number(name, i, last) + 1)
                copy(s_sb[:, 2 * s:2 * s + 2], sc_bank[SC.bank(name, i, last)][:, 0:2 * ST:2]
                     ).then_inc(sc_free, 1)
                act.wait_ge(sc_free, SC.number(name, i, last) + 1)
                for q in range(ST):
                    r = 2 * s + q
                    if not (isinstance(i, int) and i == 0 and r < 2):
                        act.wait_ge(R_sbv, 4 * i + (r - 1))
                    copy(sbv[:, q, :], bv1_b[:, :], scale=s_sb[:, r:r + 1]).then_inc(sbv_set, 1)

            def normalise(r, i, par):
                if r == 0:
                    act.wait_ge(norm_set, i + 1)
                    if not (isinstance(i, int) and i == 0):
                        act.wait_ge(y_out, 16 * i)
                nc.scalar.activation(Y[:, r, :], R[par][:, r, :], ACT.Identity, bias=nmr[:, r:r + 1],
                                     scale=rstd[:, r:r + 1]).then_inc(Y_set, 1)

            def context(i, par):
                act.wait_ge(c_in, 16 * i + 16)
                if not (isinstance(i, int) and i < 2):
                    act.wait_ge(pj_full, PJ.number("wb", i - 2) + 1)
                copy(Cs[par][0][:, :, :], C[:, :, :]).then_inc(Cs_hi, 1)

            def cT_(l, i):
                tp(f"cT{l}", i, False, cT[0][:, l, :])

            def xT_(d, i):
                tp(f"xT{d}", i, False, xT[0][:, d, :])

            def u_(l, i):
                pj(f"u{l}", i, False, uT[0][:, l, :], c0[:, l:l + 1])

            def G_(d, i, last):
                pj(f"G{d}", i, last, G[0][:, d, :], g1[:, d:d + 1])

            def flat(t, s):
                return t[:, s, :, :].rearrange("p a b -> p (a b)")

            context(0, 0)
            act.wait_ge(su_dve, 16)
            for l in range(LT):
                cT_(l, None)
            for d in range(DT):
                xT_(d, None)
            u_(0, None)
            u_(1, None)
            G_(0, None, False)
            G_(1, None, False)
            exps(0, 0, None, False, 1)
            exps(0, 1, None, False, 2)

            def body(i, par, last, first=False):
                nm = 4 * i + 2
                tp("PTa", i, last, flat(PT[0], 0))
                G_(2, i, last)
                tp("PTb", i, last, flat(PT[0], 1))
                if not last:
                    context(i + 1, 1 - par)
                G_(3, i, last)
                pj("Pa", i, last, flat(PcT[0], 0))
                if not last:
                    cT_(0, i)
                pj("Pb", i, last, flat(PcT[0], 1))
                if not last:
                    cT_(1, i)
                for r in range(4):
                    if not last:
                        xT_(r, i)
                    if not first:
                        normalise(r, i - 1, 1 - par)
                tp("yTa0", i, last, yT[0][:, 0, 0:2, :].rearrange("p a b -> p (a b)"))
                if not last:
                    u_(0, i)
                tp("yTa1", i, last, yT[0][:, 0, 2:4, :].rearrange("p a b -> p (a b)"))
                tp("yTb0", i, last, yT[0][:, 1, 0:2, :].rearrange("p a b -> p (a b)"))
                if not last:
                    u_(1, i)
                tp("yTb1", i, last, yT[0][:, 1, 2:4, :].rearrange("p a b -> p (a b)"))
                exps(1, 0, i, last, nm + 1)
                w_(0, i)
                exps(1, 1, i, last, nm + 2)
                w_(1, i)
                if not last:
                    exps(0, 0, i, last, nm + 3)
                pj("wa", i, last, flat(wcT[0], 0))
                if not last:
                    exps(0, 1, i, last, nm + 4)
                    G_(0, i, last)
                s_(0, i, last)
                pj("wb", i, last, flat(wcT[0], 1))
                if not last:
                    G_(1, i, last)
                s_(1, i, last)

            body(0, 0, False, True)
            body(1, 1, False)
            with act.Fori(1, PAIRS // 2 - 1) as j:
                body(2 * j, 0, False)
                body(2 * j + 1, 1, False)
            body(PAIRS - 2, 0, False)
            body(PAIRS - 1, 1, True)
            for r in range(4):
                normalise(r, PAIRS - 1, 1)

        @block.vector
        def _(dve):
            def minus(dst, src, hi):
                return nc.vector.tensor_tensor(dst, src, fp(hi), ALU.subtract)

            nc.vector.memset(half[:, :], -0.5)
            nc.vector.memset(ones_f[:, :], 1.0).then_inc(su_dve, 1)
            for h in range(0, HT, 2):
                dve.wait_ge(su_full, 5 + h // 2)
                nc.vector.tensor_copy(WkT[:, h:h + 2, :], bank[4 + h // 2][:, :].rearrange(
                    "p (a b) -> p a b", a=2)).then_inc(su_dve, 1)
            dve.wait_ge(b_in, 7 * 16)
            dve.wait_ge(su_dve, 1)
            nc.vector.tensor_copy(ones[:, :], ones_f[:, 0:2])
            for h in range(HT):
                nc.vector.tensor_scalar(bvw[:, h, :], ones_f[:, :], bcol[:, 1, h:h + 1], None, ALU.mult)
            for h in range(0, HT, 2):
                dve.wait_ge(su_full, 7 + h // 2)
                nc.vector.tensor_copy(WvT[:, h:h + 2, :], bank[6 + h // 2][:, :].rearrange(
                    "p (a b) -> p a b", a=2)).then_inc(su_dve, 1)
            for n in range(2):
                dve.wait_ge(su_act, 5 + n)
                nc.vector.scalar_tensor_tensor(
                    A0[1][:, 2 * n:2 * n + 2, :].rearrange("p a b -> p (a b)"), bank[n][:, :], SCALE,
                    fp(A0[0][:, 2 * n:2 * n + 2, :].rearrange("p a b -> p (a b)")),
                    ALU.mult, ALU.subtract).then_inc(su_dve, 1)
            dve.wait_ge(su_full, 11)
            nc.vector.tensor_scalar(c0[:, :], bank[2][:, 0:LT], SCALE, None, ALU.mult).then_inc(su_dve, 1)
            dve.wait_ge(su_act, 7)
            minus(Bv[1][:, 0, :], bank[4][:, :], Bv[0][:, 0, :])
            minus(Bv[1][:, 1, :], bank[5][:, :], Bv[0][:, 1, :]).then_inc(su_dve, 1)
            dve.wait_ge(su_full, 13)
            nc.vector.tensor_tensor(c1_b[:, :], bank[3][:, :], c1_b[:, :], ALU.add).then_inc(su_dve, 1)
            for h in range(0, HT, 2):
                dve.wait_ge(su_full, 18 + h // 2)
                nc.vector.tensor_copy(WkT[:, h:h + 2, :], bank[4 + h // 2][:, :].rearrange(
                    "p (a b) -> p a b", a=2)).then_inc(su_dve, 1)
            dve.wait_ge(su_act, 12)
            minus(V1[1][:, :, :], WvN, V1[0][:, :, :]).then_inc(su_dve, 1)
            for l in range(LT):
                dve.wait_ge(su_act, 13 + l)
                nc.vector.scalar_tensor_tensor(A1T[1][:, l, :], bank[6 + l][:, :], SCALE,
                                               fp(A1T[0][:, l, :]), ALU.mult, ALU.subtract
                                               ).then_inc(su_dve, 1)
            dve.wait_ge(su_full, 21)
            nc.vector.tensor_scalar(g1[:, :], bank[5][:, 0:DT], SCALE, None, ALU.mult).then_inc(su_dve, 1)
            dve.wait_ge(su_dve, 16)

            steps = [0]

            def tp(name, i, last, dst, hi):
                dve.wait_ge(tp_hi, TP.number(name, i, last) + 1)
                minus(dst, tp_bank[TP.bank(name, i, last)][:, :], hi).then_inc(tp_free, 1)

            def pj(name, i, last, dst, hi, bias=None):
                dve.wait_ge(pj_hi, PJ.number(name, i, last) + 1)
                src = pj_bank[PJ.bank(name, i, last)][:, :]
                if bias is None:
                    minus(dst, src, hi).then_inc(pj_free, 1)
                else:
                    nc.vector.scalar_tensor_tensor(dst, src, bias, fp(hi), ALU.add, ALU.subtract
                                                   ).then_inc(pj_free, 1)

            def maxima(layer, s, i, last):
                name = f"S{layer}" + "ab"[s]
                dve.wait_ge(sc_full, SC.number(name, i, last) + 1)
                nmax = nmax0 if layer == 0 else nmax1
                nc.vector.tensor_reduce(nmax[:, 2 * s:2 * s + 2],
                                        sc_bank[SC.bank(name, i, last)][:, :].rearrange("p (a b) -> p a b", a=ST),
                                        AX.X, ALU.max, negate=True).then_inc(neg_max, 1)

            def cT_(l, i):
                tp(f"cT{l}", i, False, cT[1][:, l, :], cT[0][:, l, :])

            def xT_(d, i):
                tp(f"xT{d}", i, False, xT[1][:, d, :], xT[0][:, d, :])

            def u_(l, i):
                pj(f"u{l}", i, False, uT[1][:, l, :], uT[0][:, l, :], c0[:, l:l + 1])

            def G_(d, i, last):
                pj(f"G{d}", i, last, G[1][:, d, :], G[0][:, d, :], g1[:, d:d + 1])

            def flat(t, s):
                return t[:, s, :, :].rearrange("p a b -> p (a b)")

            def yT_(s, n, i, last):
                tp(f"yT{'ab'[s]}{n}", i, last, *[yT[a][:, s, 2 * n:2 * n + 2, :].rearrange(
                    "p a b -> p (a b)") for a in (1, 0)])

            def x1(r, i, last, par):
                if r == 0:
                    sums = SC.number("S0b", None) if isinstance(i, int) and i == 0 else SC.number("S0b", i - 1)
                    dve.wait_ge(sc_free, sums + 1)
                    nc.vector.reciprocal(rz0[:, :], Z0[:, :]).then_inc(dve_step, 1)
                    dve.wait_ge(R_set, i + 1)
                    dve.wait_ge(dve_step, 7 * i + 1)
                dve.wait_ge(ot_full, OT.number(f"out{r}", i, last) + 1)
                nc.vector.scalar_tensor_tensor(R[par][:, r, :], ot_bank[OT.bank(f"out{r}", i)][:, :],
                                               rz0[:, r:r + 1], R[par][:, r, :], ALU.mult, ALU.add
                                               ).then_inc(ot_free, 1)

            def w_inv(s, i, last):
                dve.wait_ge(sc_free, SC.number("S1" + "ab"[s], i, last) + 1)
                nc.vector.reciprocal(rz1[:, 2 * s:2 * s + 2], Z1[:, 2 * s:2 * s + 2]).then_inc(rz1_set, 1)

            def w_(s, i):
                dve.wait_ge(w_hi, 2 * i + (s + 1))
                for m in range(ST):
                    r = 2 * s + m
                    done = nc.vector.scalar_tensor_tensor(w[1][:, s, m, :], E1[:, r, :], rz1[:, r:r + 1],
                                                          fp(w[0][:, s, m, :]), ALU.mult, ALU.subtract)
                done.then_inc(w_lo, 1)

            def x2(r, i, last, par):
                dve.wait_ge(ot_full, OT.number(f"pred{r}", i, last) + 1)
                dve.wait_ge(R_sbv, 4 * i + (r + 1))
                nc.vector.tensor_tensor(R[par][:, r, :], ot_bank[OT.bank(f"pred{r}", i)][:, :],
                                        R[par][:, r, :], ALU.add).then_inc(ot_free, 1)
                dve.wait_ge(ot_free, OT.number(f"pred{r}", i, last) + 1)
                nc.vector.bn_stats(stats[:, r, :], R[par][:, r, :]).then_inc(dve_step, 1)

            def variances(i):
                dve.wait_ge(dve_step, 7 * i + 5)
                nc.vector.tensor_tensor(msum[:, :, :], stats[:, :, 1:3], stats[:, :, 4:6], ALU.add)
                nc.vector.tensor_tensor(mdif[:, :], stats[:, :, 1], stats[:, :, 4], ALU.subtract
                                        ).then_inc(dve_step, 1)
                dve.wait_ge(dve_step, 7 * i + 6)
                nc.vector.scalar_tensor_tensor(msq[:, :], mdif[:, :], 0.25, mdif[:, :], ALU.mult, ALU.mult)
                nc.vector.tensor_scalar(vin[:, :], msum[:, :, 1], 1.0 / D, EPS, ALU.mult, ALU.add
                                        ).then_inc(dve_step, 1)
                dve.wait_ge(dve_step, 7 * i + 7)
                if not (isinstance(i, int) and i == 0):
                    dve.wait_ge(norm_set, i)
                nc.vector.tensor_tensor(ve[:, :], vin[:, :], msq[:, :], ALU.add)
                nc.vector.tensor_scalar(nmu[:, :], msum[:, :, 0], -0.5, None, ALU.mult).then_inc(mv_set, 1)

            for l in range(LT):
                cT_(l, None)
            for d in range(DT):
                xT_(d, None)
            u_(0, None)
            u_(1, None)
            G_(0, None, False)
            G_(1, None, False)
            maxima(0, 0, None, False)
            maxima(0, 1, None, False)

            def body(i, par, last):
                tp("PTa", i, last, flat(PT[1], 0), flat(PT[0], 0))
                G_(2, i, last)
                tp("PTb", i, last, flat(PT[1], 1), flat(PT[0], 1))
                G_(3, i, last)
                pj("Pa", i, last, flat(PcT[1], 0), flat(PcT[0], 0))
                if not last:
                    cT_(0, i)
                pj("Pb", i, last, flat(PcT[1], 1), flat(PcT[0], 1))
                if not last:
                    cT_(1, i)
                for r in range(4):
                    x1(r, i, last, par)
                    if not last:
                        xT_(r, i)
                yT_(0, 0, i, last)
                if not last:
                    u_(0, i)
                yT_(0, 1, i, last)
                yT_(1, 0, i, last)
                if not last:
                    u_(1, i)
                yT_(1, 1, i, last)
                maxima(1, 0, i, last)
                w_inv(0, i, last)
                w_(0, i)
                maxima(1, 1, i, last)
                w_inv(1, i, last)
                w_(1, i)
                if not last:
                    maxima(0, 0, i, last)
                    maxima(0, 1, i, last)
                pj("wa", i, last, flat(wcT[1], 0), flat(wcT[0], 0))
                if not last:
                    G_(0, i, last)
                pj("wb", i, last, flat(wcT[1], 1), flat(wcT[0], 1))
                if not last:
                    G_(1, i, last)
                for r in range(4):
                    x2(r, i, last, par)
                variances(i)

            body(0, 0, False)
            body(1, 1, False)
            with dve.Fori(1, PAIRS // 2 - 1) as j:
                body(2 * j, 0, False)
                body(2 * j + 1, 1, False)
            body(PAIRS - 2, 0, False)
            body(PAIRS - 1, 1, True)

        @block.gpsimd
        def _(pool):
            nc.gpsimd.memset(ident[:, :], 0.0).then_inc(const_set, 1)
            pool.wait_ge(const_set, 1)
            nc.gpsimd.affine_select(out=ident[:, :], in_=ident[:, :], compare_op=ALU.not_equal, fill=1.0,
                                    base=0, pattern=[[-1, P]], channel_multiplier=1).then_inc(const_set, 1)

            def context(i, par):
                pool.wait_ge(Cs_hi, i + 1)
                nc.gpsimd.tensor_tensor(Cs[par][1][:, :, :], C[:, :, :], fp(Cs[par][0][:, :, :]),
                                        ALU.subtract).then_inc(Cs_set, 1)

            def residual(i, par, first=False):
                pool.wait_ge(tp_full, TP.number("xT3", None if first else i - 1) + 1)
                if not (isinstance(i, int) and i < 2):
                    pool.wait_ge(Y_set, 4 * i - 4)
                for r in range(4):
                    done = nc.gpsimd.tensor_tensor(R[par][:, r, :], X[:, r, :], c1_b[:, :], ALU.add)
                done.then_inc(R_set, 1)

            def add_sbv(i, par):
                for r in range(4):
                    pool.wait_ge(sbv_set, 4 * i + (r + 1))
                    nc.gpsimd.tensor_tensor(R[par][:, r, :], R[par][:, r, :], sbv[:, r % 2, :], ALU.add
                                            ).then_inc(R_sbv, 1)

            def scales(i):
                pool.wait_ge(mv_set, i + 1)
                nc.gpsimd.tensor_tensor(rstd[:, :], ve[:, :], half[:, :], ALU.pow).then_inc(norm_step, 1)
                pool.wait_ge(norm_step, i + 1)
                nc.gpsimd.tensor_tensor(nmr[:, :], nmu[:, :], rstd[:, :], ALU.mult).then_inc(norm_set, 1)

            def finish(i):
                for r in range(5):
                    if r < 4:
                        pool.wait_ge(Y_set, 4 * i + (r + 1))
                        nc.gpsimd.tensor_tensor(Y[:, r, :], Y[:, r, :], gamma_b[:, :], ALU.mult
                                                ).then_inc(Y_mul, 1)
                    if r > 0:
                        pool.wait_ge(Y_mul, 4 * i + r)
                        done = nc.gpsimd.tensor_tensor(Y[:, r - 1, :], Y[:, r - 1, :], beta_b[:, :], ALU.add)
                done.then_inc(Y_done, 1)

            def body(i, par, first=False):
                context(i + 1, 1 - par)
                if not first:
                    scales(i - 1)
                    finish(i - 1)
                residual(i + 1, 1 - par)
                add_sbv(i, par)

            context(0, 0)
            pool.wait_ge(su_dve, 16)
            residual(0, 0, True)
            body(0, 0, True)
            body(1, 1)
            with pool.Fori(1, PAIRS // 2 - 1) as j:
                body(2 * j, 0)
                body(2 * j + 1, 1)
            body(PAIRS - 2, 0)
            scales(PAIRS - 2)
            finish(PAIRS - 2)
            add_sbv(PAIRS - 1, 1)
            scales(PAIRS - 1)
            finish(PAIRS - 1)


_INS = ["x", "ctx_512", "L0_xattn_Wq", "L0_xattn_bq", "L0_xattn_Wk", "L0_xattn_Wv", "L0_xattn_bv",
        "L0_xattn_Wo", "L0_xattn_bo", "L1_xattn_Wq", "L1_xattn_Wk", "L1_xattn_bk", "L1_xattn_Wv",
        "L1_xattn_bv", "L1_xattn_gamma", "L1_xattn_beta"]


def kernel(**inputs):
    import numpy as _np
    import concourse.bacc as _bacc
    from concourse import mybir as _mybir
    from concourse.bass_utils import run_bass_kernel_spmd as _run

    nc = _bacc.Bacc("TRN2", target_bir_lowering=False, num_devices=1)
    arrays, args = {}, []
    for name in _INS:
        a = _np.ascontiguousarray(inputs[name])
        arrays[f"in_{name}"] = a
        args.append(nc.dram_tensor(f"in_{name}", a.shape, _mybir.dt.from_np(a.dtype), kind="ExternalInput").ap())
    args.append(nc.dram_tensor("out", (NSEQ, S, D), _mybir.dt.float32, kind="ExternalOutput").ap())
    build(nc, *args)
    r = _run(nc, [arrays], core_ids=[0])
    return r.results[0]["out"]
```

```python
import concourse.bass as bass
from concourse import mybir
from contextlib import ExitStack

P = 128
NSEQ, S, D, L = 64, 256, 512, 256
H = 512
PAIRS = NSEQ // 2
DT, LT, HT, ST = D // P, L // P, H // P, S // P
W = 2 * S
SCALE = float(H) ** -0.5
EPS = 1e-6

TP_BODY = ["PTa", "PTb", "cT0", "cT1", "xT0", "xT1", "xT2", "xT3", "yTa0", "yTa1", "yTb0", "yTb1",
           "sa", "sb"]
PJ_BODY = ["G2", "G3", "Pa", "Pb", "u0", "u1", "wa", "G0", "wb", "G1"]
SC_BODY = ["S1a", "S1b", "S0a", "S0b"]
OT_BODY = ["out0", "out1", "out2", "out3", "pred0", "pred1", "pred2", "pred3"]
TP_FRONT = ["cT0", "cT1", "xT0", "xT1", "xT2", "xT3"]
PJ_FRONT = ["u0", "u1", "G0", "G1"]
SC_FRONT = ["S0a", "S0b"]


class Ring:

    def __init__(self, front, body):
        self.front, self.body = front, body
        self.last = [n for n in body if n not in front or n in ("G2", "G3")]

    def index(self, name, i, last):
        if i is None:
            return self.front.index(name)
        return (self.last if last else self.body).index(name)

    def number(self, name, i, last=False):
        if i is None:
            return self.index(name, i, last)
        return i * len(self.body) + (len(self.front) + self.index(name, i, last))

    def bank(self, name, i, last=False):
        return self.index(name, i, last) % 2


TP, PJ, SC, OT = (Ring(TP_FRONT, TP_BODY), Ring(PJ_FRONT, PJ_BODY), Ring(SC_FRONT, SC_BODY),
                  Ring([], OT_BODY))


def build(nc, x, ctxt, Wq0, bq0, Wk0, Wv0, bv0, Wo0, bo0, Wq1, Wk1, bk1, Wv1, bv1, gamma, beta, out):
    f32, f32r = mybir.dt.float32, mybir.dt.float32r
    ALU, ACT, AX = mybir.AluOpType, mybir.ActivationFunctionType, mybir.AxisListType

    x_v = x.rearrange("(n s) (p q) d -> n p s (q d)", s=2, q=ST)
    c_v = ctxt.rearrange("(n s) (p q) d -> n p s (q d)", s=2, q=ST)
    o_v = out.rearrange("(n s) (p q) d -> n p s (q d)", s=2, q=ST)

    with ExitStack() as stack:
        def sb(name, shape, dt=f32):
            return stack.enter_context(nc.sbuf_tensor(name, shape, dt))

        def split(name, shape):
            return [sb(name + "_hi", shape, f32r), sb(name + "_lo", shape, f32r)]

        def sem(name):
            return stack.enter_context(nc.semaphore(name))

        ident = sb("ident", [P, P])
        A0 = split("A0", [P, DT, L])
        Bv = split("Bv", [P, LT, D])
        A1T = split("A1T", [P, LT, D])
        V1 = split("V1", [P, LT, D])
        pick = sb("pick", [P, P], f32r)
        pick_f = sb("pick_f", [P, P])
        ones_f = sb("ones_f", [P, P])
        bvK = sb("bvK", [P, D], f32r)
        c0 = sb("c0", [P, LT])
        g1 = sb("g1", [P, DT])
        c1_b = sb("c1_b", [P, D])
        bv1_b = sb("bv1_b", [P, D])
        gamma_b = sb("gamma_b", [P, D])
        beta_b = sb("beta_b", [P, D])
        bcol = sb("bcol", [P, 3, HT])
        half = sb("half", [P, 2 * ST])

        X = sb("X", [P, 2 * ST, D])
        R = [sb(f"R{n}", [P, 2 * ST, D]) for n in range(2)]
        Y = sb("Y", [P, 2 * ST, D])
        C = sb("C", [P, 2 * ST, L])
        Cs = [split(f"C{n}", [P, 2 * ST, L]) for n in range(2)]
        cT = split("cT", [P, LT, W])
        xT = split("xT", [P, DT, W])
        uT = split("uT", [P, LT, W])
        G = split("G", [P, DT, W])
        E0 = sb("E0", [P, 2 * ST, S])
        PT = split("PT", [P, 2, ST, S])
        PcT = split("PcT", [P, 2, LT, S])
        yT = split("yT", [P, 2, DT, S])
        E1 = sb("E1", [P, 2 * ST, S])
        w = split("w", [P, 2, ST, S])
        wcT = split("wcT", [P, 2, LT, S])
        srow = sb("srow", [P, 2, S], f32r)
        nmax0, Z0, rz0 = sb("nmax0", [P, 4]), sb("Z0", [P, 4]), sb("rz0", [P, 4])
        nmax1, Z1, rz1 = sb("nmax1", [P, 4]), sb("Z1", [P, 4]), sb("rz1", [P, 4])
        stats = sb("stats", [P, 4, 6])
        msum = sb("msum", [P, 4, 2])
        mdif, msq, vin = (sb(n, [P, 4]) for n in ("mdif", "msq", "vin"))
        ve, rstd, nmu, nmr = (sb(n, [P, 4]) for n in ("ve", "rstd", "nmu", "nmr"))

        bank = [stack.enter_context(nc.psum_tensor(f"bank{n}", [P, 512], f32)) for n in range(8)]
        tp_bank, pj_bank, sc_bank, ot_bank = bank[0:2], bank[2:4], bank[4:6], bank[6:8]

        w_in = [sem(f"w_in{n}") for n in range(7)]
        b_in = sem("b_in")
        const_set = sem("const_set")
        su_full = sem("su_full")
        su_act, su_dve = sem("su_act"), sem("su_dve")
        x_in, c_in, y_out = sem("x_in"), sem("c_in"), sem("y_out")
        tp_full, tp_hi, tp_free = sem("tp_full"), sem("tp_hi"), sem("tp_free")
        pj_full, pj_hi, pj_free = sem("pj_full"), sem("pj_hi"), sem("pj_free")
        sc_full, sc_free = sem("sc_full"), sem("sc_free")
        ot_full, ot_free = sem("ot_full"), sem("ot_free")
        neg_max = sem("neg_max")
        rz1_set = sem("rz1_set")
        w_hi, w_lo = sem("w_hi"), sem("w_lo")
        Cs_set = sem("Cs_set")
        R_set = sem("R_set")
        mv_set = sem("mv_set")
        norm_set = sem("norm_set")
        Y_set = sem("Y_set")
        Y_mul = sem("Y_mul")
        Y_done = sem("Y_done")
        Cs_hi = sem("Cs_hi")
        norm_step = sem("norm_step")
        rz0_set = sem("rz0_set")
        ln_step = sem("ln_step")

        XS = X[:, :, :].rearrange("p a b -> p (a b)")
        WqN = R[0][:, :, :]
        WqT = R[1][:, :, :]
        WkN = E0[:, :, :].rearrange("p a b -> p (a b)").rearrange("p (t n) -> p t n", t=LT)
        WkT = E1[:, :, :]
        WvN = C[:, :, :].rearrange("p a b -> p (a b)").rearrange("p (t n) -> p t n", t=LT)
        WvT = XS[:, 0:HT * L].rearrange("p (t n) -> p t n", t=HT)
        WoN = Y[:, :, :]
        bvw = XS[:, HT * L:HT * L + HT * P].rearrange("p (t n) -> p t n", t=HT)

        block = stack.enter_context(nc.Block())

        def fp(ap):
            return ap.bitcast(f32)

        @block.sync
        def _(sp):
            def rows(a):
                return a.rearrange("(t p) n -> p t n", p=P)

            sp.dma_start(WqN, rows(Wq0)).then_inc(w_in[0], 16)
            sp.dma_start(WkN, rows(Wk0)).then_inc(w_in[1], 16)
            sp.dma_start(WvN, rows(Wv0)).then_inc(w_in[2], 16)
            sp.dma_start(WoN, Wo0.rearrange("(p t) n -> p t n", p=P)).then_inc(w_in[3], 16)
            sp.wait_ge(su_full, 6)
            sp.dma_start(WqN, rows(Wq1)).then_inc(w_in[4], 16)
            sp.dma_start(WkN, rows(Wk1)).then_inc(w_in[5], 16)
            sp.wait_ge(su_full, 8)
            sp.dma_start(WvN, rows(Wv1)).then_inc(w_in[6], 16)
            sp.wait_ge(su_dve, 13)
            sp.dma_start(C[:, :, :].rearrange("p (s q) l -> p s (q l)", s=2), c_v[0]).then_inc(c_in, 16)
            sp.wait_ge(su_full, 13)
            sp.dma_start(X[:, :, :].rearrange("p (s q) d -> p s (q d)", s=2), x_v[0]).then_inc(x_in, 16)

            def load(n):
                first = isinstance(n, int) and n == 1
                sp.wait_ge(tp_full, TP.number("cT1", None if first else n - 2) + 1)
                sp.wait_ge(Cs_set, n)
                sp.dma_start(C[:, :, :].rearrange("p (s q) l -> p s (q l)", s=2), c_v[n]).then_inc(c_in, 16)
                sp.wait_ge(R_set, n)
                sp.dma_start(X[:, :, :].rearrange("p (s q) d -> p s (q d)", s=2), x_v[n]).then_inc(x_in, 16)

            def store(i):
                sp.wait_ge(Y_done, i + 1)
                sp.dma_start(o_v[i], Y[:, :, :].rearrange("p (s q) d -> p s (q d)", s=2)).then_inc(y_out, 16)

            load(1)
            load(2)
            with sp.Fori(3, PAIRS) as n:
                load(n)
                store(n - 3)
            for n in range(PAIRS - 3, PAIRS):
                store(n)
            sp.wait_ge(y_out, 16 * PAIRS)

        @block.tensor
        def _(pe):
            def product(dst, stat, mov, k, first=True):
                for t in range(k):
                    for n, (a, b) in enumerate(((0, 0), (0, 1), (1, 0))):
                        last = nc.tensor.matmul(dst, stat(a, t), mov(b, t), start=(first and t == 0 and n == 0),
                                                stop=(t == k - 1 and n == 2))
                return last

            def transposes(dst, src):
                for n, s in enumerate(src):
                    last = nc.tensor.transpose(dst[:, n * P:(n + 1) * P], s, ident[:, :])
                return last

            pe.wait_ge(const_set, 2)
            pe.wait_ge(w_in[0], 16)
            for h in range(HT):
                transposes(bank[h], [WqN[:, d, h::HT] for d in range(DT)]).then_inc(su_full, 1)
            pe.wait_ge(w_in[1], 16)
            for h in range(0, HT, 2):
                transposes(bank[4 + h // 2], [WkN[:, l, k::HT] for k in (h, h + 1)
                                              for l in range(LT)]).then_inc(su_full, 1)
            pe.wait_ge(w_in[2], 16)
            for h in range(0, HT, 2):
                transposes(bank[6 + h // 2], [WvN[:, l, k::HT] for k in (h, h + 1)
                                              for l in range(LT)]).then_inc(su_full, 1)
            pe.wait_ge(su_act, 4)
            pe.wait_ge(su_dve, 3)
            for d in range(0, DT, 2):
                for k in (d, d + 1):
                    for h in range(HT):
                        last = nc.tensor.matmul(bank[d // 2][:, (k - d) * L:(k - d + 1) * L],
                                                WqT[:, h, k * P:(k + 1) * P], WkT[:, h, :],
                                                start=(h == 0), stop=(h == HT - 1))
                last.then_inc(su_full, 1)
            pe.wait_ge(b_in, 7 * 16)
            for l in range(LT):
                for h in range(HT):
                    last = nc.tensor.matmul(bank[2][:, l:l + 1], WkT[:, h, l * P:(l + 1) * P],
                                            bcol[:, 0, h:h + 1], start=(h == 0), stop=(h == HT - 1))
            last.then_inc(su_full, 1)
            pe.wait_ge(su_dve, 5)
            pe.wait_ge(w_in[3], 16)
            for l in range(LT):
                for h in range(HT):
                    last = nc.tensor.matmul(bank[4 + l][:, :], WvT[:, h, l * P:(l + 1) * P], WoN[:, h, :],
                                            start=(h == 0), stop=(h == HT - 1))
            last.then_inc(su_full, 1)
            for h in range(HT):
                last = nc.tensor.matmul(bank[3][:, :], bvw[:, h, :], WoN[:, h, :],
                                        start=(h == 0), stop=(h == HT - 1))
            last.then_inc(su_full, 1)
            pe.wait_ge(su_dve, 10)
            pe.wait_ge(w_in[4], 16)
            for h in range(HT):
                transposes(bank[h], [WqN[:, d, h::HT] for d in range(DT)]).then_inc(su_full, 1)
            pe.wait_ge(w_in[5], 16)
            for h in range(0, HT, 2):
                transposes(bank[4 + h // 2], [WkN[:, l, k::HT] for k in (h, h + 1)
                                              for l in range(LT)]).then_inc(su_full, 1)
            pe.wait_ge(su_act, 11)
            pe.wait_ge(su_dve, 12)
            for l in range(LT):
                for h in range(HT):
                    last = nc.tensor.matmul(bank[6 + l][:, :], WkT[:, h, l * P:(l + 1) * P], WqT[:, h, :],
                                            start=(h == 0), stop=(h == HT - 1))
            last.then_inc(su_full, 1)
            for d in range(DT):
                for h in range(HT):
                    last = nc.tensor.matmul(bank[5][:, d:d + 1], WqT[:, h, d * P:(d + 1) * P],
                                            bcol[:, 2, h:h + 1], start=(h == 0), stop=(h == HT - 1))
            last.then_inc(su_full, 1)
            pe.wait_ge(su_dve, 17)

            def take(ring, name, i, last, free):
                k = ring.number(name, i, last)
                if not (isinstance(k, int) and k < 2):
                    pe.wait_ge(free, k - 1)

            def tp(name, i, last, src):
                take(TP, name, i, last, tp_free)
                transposes(tp_bank[TP.bank(name, i, last)], src).then_inc(tp_full, 1)

            def tp_ready(name, i, last):
                pe.wait_ge(tp_free, TP.number(name, i, last) + 1)

            def pj_ready(name, i, last):
                pe.wait_ge(pj_free, PJ.number(name, i, last) + 1)

            def cT_(l, i):
                tp(f"cT{l}", i, False, [C[:, r, l * P:(l + 1) * P] for r in range(4)])

            def xT_(d, i):
                tp(f"xT{d}", i, False, [X[:, r, d * P:(d + 1) * P] for r in range(4)])

            def u_(l, i):
                take(PJ, f"u{l}", i, False, pj_free)
                product(pj_bank[PJ.bank(f"u{l}", i)][:, :], lambda a, t: A0[a][:, t, l * P:(l + 1) * P],
                        lambda b, t: xT[b][:, t, :], DT).then_inc(pj_full, 1)

            def G_(d, i, last):
                take(PJ, f"G{d}", i, last, pj_free)
                product(pj_bank[PJ.bank(f"G{d}", i, last)][:, :],
                        lambda a, t: A1T[a][:, t, d * P:(d + 1) * P],
                        lambda b, t: cT[b][:, t, :], LT).then_inc(pj_full, 1)

            def S0_(s, i):
                name = "S0" + "ab"[s]
                take(SC, name, i, False, sc_free)
                for q in range(ST):
                    r = s * S + q * P
                    last = product(sc_bank[SC.bank(name, i)][:, q * S:(q + 1) * S],
                                   lambda a, t: uT[a][:, t, r:r + P],
                                   lambda b, t: cT[b][:, t, s * S:(s + 1) * S], LT)
                last.then_inc(sc_full, 1)

            def PT_(s, i, last):
                name = "PT" + "ab"[s]
                if isinstance(i, int) and i == 0:
                    pe.wait_ge(sc_free, SC.number("S0" + "ab"[s], None) + 1)
                else:
                    pe.wait_ge(sc_free, SC.number("S0" + "ab"[s], i - 1) + 1)
                tp(name, i, last, [E0[:, 2 * s + q, k * P:(k + 1) * P] for k in range(ST) for q in range(ST)])

            def Pc_(s, i, last, par):
                name = "P" + "ab"[s]
                tp_ready("PT" + "ab"[s], i, last)
                if s == 0:
                    pe.wait_ge(Cs_set, i + 1)
                take(PJ, name, i, last, pj_free)
                for l in range(LT):
                    done = product(pj_bank[PJ.bank(name, i, last)][:, l * S:(l + 1) * S],
                                   lambda a, t: Cs[par][a][:, 2 * s + t, l * P:(l + 1) * P],
                                   lambda b, t: PT[b][:, s, t, :], ST)
                done.then_inc(pj_full, 1)

            def out_(r, i, last):
                s, q = divmod(r, ST)
                if q == 0:
                    pj_ready("P" + "ab"[s], i, last)
                take(OT, f"out{r}", i, last, ot_free)
                product(ot_bank[OT.bank(f"out{r}", i)][:, :], lambda a, t: PcT[a][:, s, t, q * P:(q + 1) * P],
                        lambda b, t: Bv[b][:, t, :], LT).then_inc(ot_full, 1)

            def yT_(s, n, i, last):
                pe.wait_ge(ot_free, OT.number(f"out{2 * s + 1}", i, last) + 1)
                tp(f"yT{'ab'[s]}{n}", i, last, [R_(i, last)[:, 2 * s + q, d * P:(d + 1) * P]
                                                for d in (2 * n, 2 * n + 1) for q in range(ST)])

            def S1_(s, i, last):
                name = "S1" + "ab"[s]
                tp_ready(f"yT{'ab'[s]}1", i, last)
                take(SC, name, i, last, sc_free)
                if s == 0:
                    pj_ready("G3", i, last)
                for m in range(ST):
                    c = s * S + m * P
                    done = product(sc_bank[SC.bank(name, i, last)][:, m * S:(m + 1) * S],
                                   lambda a, t: G[a][:, t, c:c + P],
                                   lambda b, t: yT[b][:, s, t, :], DT)
                done.then_inc(sc_full, 1)

            def wc_(s, i, last, par):
                name = "w" + "ab"[s]
                pe.wait_ge(w_lo, 2 * i + (s + 1))
                take(PJ, name, i, last, pj_free)
                for l in range(LT):
                    done = product(pj_bank[PJ.bank(name, i, last)][:, l * S:(l + 1) * S],
                                   lambda a, t: Cs[par][a][:, 2 * s + t, l * P:(l + 1) * P],
                                   lambda b, t: w[b][:, s, t, :], ST)
                done.then_inc(pj_full, 1)

            def s_(s, i, last):
                name = "s" + "ab"[s]
                take(TP, name, i, last, tp_free)
                dst = tp_bank[TP.bank(name, i, last)][:, 0:S]
                for t in range(ST):
                    for b in range(2):
                        done = nc.tensor.matmul(dst, pick[:, :], w[b][:, s, t, :], start=(t == 0 and b == 0),
                                                stop=(t == ST - 1 and b == 1))
                done.then_inc(tp_full, 1)

            def pred_(r, i, last):
                s, q = divmod(r, ST)
                if q == 0:
                    pj_ready("w" + "ab"[s], i, last)
                    tp_ready("s" + "ab"[s], i, last)
                take(OT, f"pred{r}", i, last, ot_free)
                dst = ot_bank[OT.bank(f"pred{r}", i)][:, :]
                nc.tensor.matmul(dst, srow[:, s, q * P:(q + 1) * P], bvK[:, :], start=True, stop=False)
                product(dst, lambda a, t: wcT[a][:, s, t, q * P:(q + 1) * P],
                        lambda b, t: V1[b][:, t, :], LT, first=False).then_inc(ot_full, 1)

            R_now = [None]

            def R_(i, last):
                return R_now[0]

            pe.wait_ge(c_in, 16)
            cT_(0, None)
            cT_(1, None)
            pe.wait_ge(x_in, 16)
            for d in range(DT):
                xT_(d, None)
            tp_ready("xT3", None, False)
            u_(0, None)
            u_(1, None)
            G_(0, None, False)
            G_(1, None, False)
            pj_ready("u1", None, False)
            S0_(0, None)
            S0_(1, None)

            def body(i, par, last):
                R_now[0] = R[par]
                PT_(0, i, last)
                G_(2, i, last)
                PT_(1, i, last)
                G_(3, i, last)
                if not last:
                    pe.wait_ge(c_in, 16 * i + 32)
                    cT_(0, i)
                Pc_(0, i, last, par)
                if not last:
                    cT_(1, i)
                Pc_(1, i, last, par)
                if not last:
                    pe.wait_ge(x_in, 16 * i + 32)
                for r in range(4):
                    if not last:
                        xT_(r, i)
                    out_(r, i, last)
                yT_(0, 0, i, last)
                yT_(0, 1, i, last)
                if not last:
                    tp_ready("xT3", i, last)
                    u_(0, i)
                yT_(1, 0, i, last)
                S1_(0, i, last)
                yT_(1, 1, i, last)
                if not last:
                    u_(1, i)
                S1_(1, i, last)
                wc_(0, i, last, par)
                if not last:
                    pj_ready("u1", i, last)
                    S0_(0, i)
                    S0_(1, i)
                    G_(0, i, last)
                s_(0, i, last)
                wc_(1, i, last, par)
                s_(1, i, last)
                if not last:
                    G_(1, i, last)
                for r in range(4):
                    pred_(r, i, last)

            body(0, 0, False)
            body(1, 1, False)
            with pe.Fori(1, PAIRS // 2 - 1) as j:
                body(2 * j, 0, False)
                body(2 * j + 1, 1, False)
            body(PAIRS - 2, 0, False)
            body(PAIRS - 1, 1, True)

        @block.scalar
        def _(act):
            def copy(dst, src, **kw):
                return nc.scalar.activation(dst, src, ACT.Copy, **kw)

            for n, v in enumerate((bq0, bv0, bk1)):
                act.dma_start(bcol[:, n, :], v.rearrange("(p t) -> p t", p=P)).then_inc(b_in, 16)
            for dst, v in ((c1_b, bo0), (bv1_b, bv1), (gamma_b, gamma), (beta_b, beta)):
                act.dma_start(dst[:, :], v.rearrange("(a n) -> a n", a=1).to_broadcast([P, D])
                              ).then_inc(b_in, 16)
            for h in range(HT):
                act.wait_ge(su_full, h + 1)
                copy(WqT[:, h, :], bank[h][:, :]).then_inc(su_act, 1)
            act.wait_ge(su_full, 10)
            for n in range(2):
                copy(A0[0][:, 2 * n:2 * n + 2, :], bank[n][:, :].rearrange("p (a b) -> p a b", a=2),
                     scale=SCALE).then_inc(su_act, 1)
            act.wait_ge(su_full, 12)
            copy(Bv[0][:, 0, :], bank[4][:, :])
            copy(Bv[0][:, 1, :], bank[5][:, :]).then_inc(su_act, 1)
            for h in range(HT):
                act.wait_ge(su_full, 14 + h)
                copy(WqT[:, h, :], bank[h][:, :]).then_inc(su_act, 1)
            act.wait_ge(w_in[6], 16)
            copy(V1[0][:, :, :], WvN).then_inc(su_act, 1)
            act.wait_ge(su_full, 20)
            for l in range(LT):
                copy(A1T[0][:, l, :], bank[6 + l][:, :], scale=SCALE).then_inc(su_act, 1)

            def tp(name, i, last, dst, cols=slice(0, 512)):
                k = TP.number(name, i, last)
                act.wait_ge(tp_full, k + 1)
                copy(dst, tp_bank[TP.bank(name, i, last)][:, cols]).then_inc(tp_hi, 1)

            def pj(name, i, last, dst, bias=None):
                k = PJ.number(name, i, last)
                act.wait_ge(pj_full, k + 1)
                src = pj_bank[PJ.bank(name, i, last)][:, :]
                if bias is None:
                    copy(dst, src).then_inc(pj_hi, 1)
                else:
                    nc.scalar.activation(dst, src, ACT.Identity, bias=bias).then_inc(pj_hi, 1)

            def exps(layer, s, i, last):
                name = f"S{layer}" + "ab"[s]
                E, Z, nmax = (E0, Z0, nmax0) if layer == 0 else (E1, Z1, nmax1)
                act.wait_ge(neg_max, SC.number(name, i, last) + 1)
                for q in range(ST):
                    r = 2 * s + q
                    done = nc.scalar.activation(E[:, r, :],
                                                sc_bank[SC.bank(name, i, last)][:, q * S:(q + 1) * S],
                                                ACT.Exp, bias=nmax[:, r:r + 1], accum_out=Z[:, r:r + 1])
                done.then_inc(sc_free, 1)

            def w_(s, i):
                act.wait_ge(rz1_set, 2 * i + (s + 1))
                for m in range(ST):
                    r = 2 * s + m
                    done = copy(w[0][:, s, m, :], E1[:, r, :], scale=rz1[:, r:r + 1])
                done.then_inc(w_hi, 1)

            def s_(s, i, last):
                tp("s" + "ab"[s], i, last, srow[:, s, :], slice(0, S))

            def normalise(r, i, par):
                if r == 0:
                    act.wait_ge(norm_set, i + 1)
                    if not (isinstance(i, int) and i == 0):
                        act.wait_ge(y_out, 16 * i)
                nc.scalar.activation(Y[:, r, :], R[par][:, r, :], ACT.Identity, bias=nmr[:, r:r + 1],
                                     scale=rstd[:, r:r + 1]).then_inc(Y_set, 1)

            def context(i, par):
                act.wait_ge(c_in, 16 * i + 16)
                if not (isinstance(i, int) and i < 2):
                    act.wait_ge(pj_full, PJ.number("wb", i - 2) + 1)
                copy(Cs[par][0][:, :, :], C[:, :, :]).then_inc(Cs_hi, 1)

            def cT_(l, i):
                tp(f"cT{l}", i, False, cT[0][:, l, :])

            def xT_(d, i):
                tp(f"xT{d}", i, False, xT[0][:, d, :])

            def u_(l, i):
                pj(f"u{l}", i, False, uT[0][:, l, :], c0[:, l:l + 1])

            def G_(d, i, last):
                pj(f"G{d}", i, last, G[0][:, d, :], g1[:, d:d + 1])

            def flat(t, s):
                return t[:, s, :, :].rearrange("p a b -> p (a b)")

            def yT_(s, n, i, last):
                tp(f"yT{'ab'[s]}{n}", i, last, yT[0][:, s, 2 * n:2 * n + 2, :].rearrange("p a b -> p (a b)"))

            act.wait_ge(b_in, 7 * 16)
            for r in (0, 32):
                copy(bvK[r:r + 1, :], bv1_b[r:r + 1, :])
            copy(w[0][64:65, :, :, :].rearrange("p a b c -> p (a b c)")[:, 0:D], bv1_b[64:65, :]
                 ).then_inc(su_act, 1)
            context(0, 0)
            act.wait_ge(su_dve, 17)
            for l in range(LT):
                cT_(l, None)
            for d in range(DT):
                xT_(d, None)
            u_(0, None)
            u_(1, None)
            G_(0, None, False)
            G_(1, None, False)
            exps(0, 0, None, False)
            exps(0, 1, None, False)

            def body(i, par, last, first=False):
                tp("PTa", i, last, flat(PT[0], 0))
                G_(2, i, last)
                tp("PTb", i, last, flat(PT[0], 1))
                G_(3, i, last)
                if not last:
                    cT_(0, i)
                pj("Pa", i, last, flat(PcT[0], 0))
                if not last:
                    cT_(1, i)
                    context(i + 1, 1 - par)
                pj("Pb", i, last, flat(PcT[0], 1))
                if not last:
                    for d in range(DT):
                        xT_(d, i)
                yT_(0, 0, i, last)
                yT_(0, 1, i, last)
                if not last:
                    u_(0, i)
                yT_(1, 0, i, last)
                if not first:
                    for r in range(3):
                        normalise(r, i - 1, 1 - par)
                exps(1, 0, i, last)
                yT_(1, 1, i, last)
                w_(0, i)
                if not last:
                    u_(1, i)
                if not first:
                    normalise(3, i - 1, 1 - par)
                exps(1, 1, i, last)
                pj("wa", i, last, flat(wcT[0], 0))
                w_(1, i)
                if not last:
                    exps(0, 0, i, last)
                    G_(0, i, last)
                    exps(0, 1, i, last)
                s_(0, i, last)
                pj("wb", i, last, flat(wcT[0], 1))
                s_(1, i, last)
                if not last:
                    G_(1, i, last)

            body(0, 0, False, True)
            body(1, 1, False)
            with act.Fori(1, PAIRS // 2 - 1) as j:
                body(2 * j, 0, False)
                body(2 * j + 1, 1, False)
            body(PAIRS - 2, 0, False)
            body(PAIRS - 1, 1, True)
            for r in range(4):
                normalise(r, PAIRS - 1, 1)

        @block.vector
        def _(dve):
            def minus(dst, src, hi):
                return nc.vector.tensor_tensor(dst, src, fp(hi), ALU.subtract)

            nc.vector.memset(half[:, :], -0.5)
            for c in (0, 32, 64):
                nc.vector.memset(pick_f[:, c:c + 1], 1.0)
                nc.vector.memset(pick_f[:, c + 1:c + 32 if c < 64 else P], 0.0)
            nc.vector.memset(fp(bvK[:, :]), 0.0)
            nc.vector.memset(ones_f[:, :], 1.0).then_inc(su_dve, 1)
            for h in range(0, HT, 2):
                dve.wait_ge(su_full, 5 + h // 2)
                nc.vector.tensor_copy(WkT[:, h:h + 2, :], bank[4 + h // 2][:, :].rearrange(
                    "p (a b) -> p a b", a=2)).then_inc(su_dve, 1)
            dve.wait_ge(b_in, 7 * 16)
            dve.wait_ge(su_dve, 1)
            nc.vector.tensor_copy(pick[:, :], pick_f[:, :])
            for h in range(HT):
                nc.vector.tensor_scalar(bvw[:, h, :], ones_f[:, :], bcol[:, 1, h:h + 1], None, ALU.mult)
            for h in range(0, HT, 2):
                dve.wait_ge(su_full, 7 + h // 2)
                nc.vector.tensor_copy(WvT[:, h:h + 2, :], bank[6 + h // 2][:, :].rearrange(
                    "p (a b) -> p a b", a=2)).then_inc(su_dve, 1)
            for n in range(2):
                dve.wait_ge(su_act, 5 + n)
                nc.vector.scalar_tensor_tensor(
                    A0[1][:, 2 * n:2 * n + 2, :].rearrange("p a b -> p (a b)"), bank[n][:, :], SCALE,
                    fp(A0[0][:, 2 * n:2 * n + 2, :].rearrange("p a b -> p (a b)")),
                    ALU.mult, ALU.subtract).then_inc(su_dve, 1)
            dve.wait_ge(su_full, 11)
            nc.vector.tensor_scalar(c0[:, :], bank[2][:, 0:LT], SCALE, None, ALU.mult).then_inc(su_dve, 1)
            dve.wait_ge(su_act, 7)
            minus(Bv[1][:, 0, :], bank[4][:, :], Bv[0][:, 0, :])
            minus(Bv[1][:, 1, :], bank[5][:, :], Bv[0][:, 1, :]).then_inc(su_dve, 1)
            dve.wait_ge(su_full, 13)
            nc.vector.tensor_tensor(c1_b[:, :], bank[3][:, :], c1_b[:, :], ALU.add).then_inc(su_dve, 1)
            for h in range(0, HT, 2):
                dve.wait_ge(su_full, 18 + h // 2)
                nc.vector.tensor_copy(WkT[:, h:h + 2, :], bank[4 + h // 2][:, :].rearrange(
                    "p (a b) -> p a b", a=2)).then_inc(su_dve, 1)
            dve.wait_ge(su_act, 12)
            minus(V1[1][:, :, :], WvN, V1[0][:, :, :]).then_inc(su_dve, 1)
            for l in range(LT):
                dve.wait_ge(su_act, 13 + l)
                nc.vector.scalar_tensor_tensor(A1T[1][:, l, :], bank[6 + l][:, :], SCALE,
                                               fp(A1T[0][:, l, :]), ALU.mult, ALU.subtract
                                               ).then_inc(su_dve, 1)
            dve.wait_ge(su_full, 21)
            nc.vector.tensor_scalar(g1[:, :], bank[5][:, 0:DT], SCALE, None, ALU.mult).then_inc(su_dve, 1)
            dve.wait_ge(su_act, 15)
            nc.vector.tensor_tensor(bvK[64:65, :], bv1_b[64:65, :],
                                    fp(w[0][64:65, :, :, :].rearrange("p a b c -> p (a b c)")[:, 0:D]),
                                    ALU.subtract).then_inc(su_dve, 1)
            dve.wait_ge(su_dve, 17)

            def tp(name, i, last, dst, hi):
                dve.wait_ge(tp_hi, TP.number(name, i, last) + 1)
                minus(dst, tp_bank[TP.bank(name, i, last)][:, :], hi).then_inc(tp_free, 1)

            def pj(name, i, last, dst, hi, bias=None):
                dve.wait_ge(pj_hi, PJ.number(name, i, last) + 1)
                src = pj_bank[PJ.bank(name, i, last)][:, :]
                if bias is None:
                    minus(dst, src, hi).then_inc(pj_free, 1)
                else:
                    nc.vector.scalar_tensor_tensor(dst, src, bias, fp(hi), ALU.add, ALU.subtract
                                                   ).then_inc(pj_free, 1)

            def maxima(layer, s, i, last):
                name = f"S{layer}" + "ab"[s]
                dve.wait_ge(sc_full, SC.number(name, i, last) + 1)
                nmax = nmax0 if layer == 0 else nmax1
                nc.vector.tensor_reduce(nmax[:, 2 * s:2 * s + 2],
                                        sc_bank[SC.bank(name, i, last)][:, :].rearrange("p (a b) -> p a b", a=ST),
                                        AX.X, ALU.max, negate=True).then_inc(neg_max, 1)

            def cT_(l, i):
                tp(f"cT{l}", i, False, cT[1][:, l, :], cT[0][:, l, :])

            def xT_(d, i):
                tp(f"xT{d}", i, False, xT[1][:, d, :], xT[0][:, d, :])

            def u_(l, i):
                pj(f"u{l}", i, False, uT[1][:, l, :], uT[0][:, l, :], c0[:, l:l + 1])

            def G_(d, i, last):
                pj(f"G{d}", i, last, G[1][:, d, :], G[0][:, d, :], g1[:, d:d + 1])

            def flat(t, s):
                return t[:, s, :, :].rearrange("p a b -> p (a b)")

            def s_(s, i, last):
                name = "s" + "ab"[s]
                dve.wait_ge(tp_hi, TP.number(name, i, last) + 1)
                minus(srow[32:33, s, :], tp_bank[TP.bank(name, i, last)][32:33, 0:S], srow[32:33, s, :]
                      ).then_inc(tp_free, 1)

            def yT_(s, n, i, last):
                tp(f"yT{'ab'[s]}{n}", i, last, *[yT[a][:, s, 2 * n:2 * n + 2, :].rearrange(
                    "p a b -> p (a b)") for a in (1, 0)])

            def P_inv(i):
                sums = SC.number("S0b", None) if isinstance(i, int) and i == 0 else SC.number("S0b", i - 1)
                dve.wait_ge(sc_free, sums + 1)
                nc.vector.reciprocal(rz0[:, :], Z0[:, :]).then_inc(rz0_set, 1)

            def x1(r, i, last, par):
                if r == 0:
                    dve.wait_ge(R_set, i + 1)
                    dve.wait_ge(rz0_set, i + 1)
                dve.wait_ge(ot_full, OT.number(f"out{r}", i, last) + 1)
                nc.vector.scalar_tensor_tensor(R[par][:, r, :], ot_bank[OT.bank(f"out{r}", i)][:, :],
                                               rz0[:, r:r + 1], R[par][:, r, :], ALU.mult, ALU.add
                                               ).then_inc(ot_free, 1)

            def w_inv(s, i, last):
                dve.wait_ge(sc_free, SC.number("S1" + "ab"[s], i, last) + 1)
                nc.vector.reciprocal(rz1[:, 2 * s:2 * s + 2], Z1[:, 2 * s:2 * s + 2]).then_inc(rz1_set, 1)

            def w_(s, i):
                dve.wait_ge(w_hi, 2 * i + (s + 1))
                for m in range(ST):
                    r = 2 * s + m
                    done = nc.vector.scalar_tensor_tensor(w[1][:, s, m, :], E1[:, r, :], rz1[:, r:r + 1],
                                                          fp(w[0][:, s, m, :]), ALU.mult, ALU.subtract)
                done.then_inc(w_lo, 1)

            def x2(r, i, last, par):
                dve.wait_ge(ot_full, OT.number(f"pred{r}", i, last) + 1)
                nc.vector.tensor_tensor(R[par][:, r, :], ot_bank[OT.bank(f"pred{r}", i)][:, :],
                                        R[par][:, r, :], ALU.add).then_inc(ot_free, 1)

            def statistics(r, i, par):
                if r == 0:
                    dve.wait_ge(ot_free, 8 * i + 8)
                nc.vector.bn_stats(stats[:, r, :], R[par][:, r, :]).then_inc(ln_step, 1)

            def variances(i):
                dve.wait_ge(ln_step, 6 * i + 4)
                nc.vector.tensor_tensor(msum[:, :, :], stats[:, :, 1:3], stats[:, :, 4:6], ALU.add)
                nc.vector.tensor_tensor(mdif[:, :], stats[:, :, 1], stats[:, :, 4], ALU.subtract
                                        ).then_inc(ln_step, 1)
                dve.wait_ge(ln_step, 6 * i + 5)
                nc.vector.scalar_tensor_tensor(msq[:, :], mdif[:, :], 0.25, mdif[:, :], ALU.mult, ALU.mult)
                nc.vector.tensor_scalar(vin[:, :], msum[:, :, 1], 1.0 / D, EPS, ALU.mult, ALU.add
                                        ).then_inc(ln_step, 1)
                dve.wait_ge(ln_step, 6 * i + 6)
                if not (isinstance(i, int) and i == 0):
                    dve.wait_ge(norm_set, i)
                nc.vector.tensor_tensor(ve[:, :], vin[:, :], msq[:, :], ALU.add)
                nc.vector.tensor_scalar(nmu[:, :], msum[:, :, 0], -0.5, None, ALU.mult).then_inc(mv_set, 1)

            for l in range(LT):
                cT_(l, None)
            for d in range(DT):
                xT_(d, None)
            u_(0, None)
            u_(1, None)
            G_(0, None, False)
            G_(1, None, False)
            maxima(0, 0, None, False)
            maxima(0, 1, None, False)

            def body(i, par, last, first=False):
                tp("PTa", i, last, flat(PT[1], 0), flat(PT[0], 0))
                G_(2, i, last)
                tp("PTb", i, last, flat(PT[1], 1), flat(PT[0], 1))
                P_inv(i)
                if not first:
                    statistics(0, i - 1, 1 - par)
                G_(3, i, last)
                if not last:
                    cT_(0, i)
                if not first:
                    statistics(1, i - 1, 1 - par)
                pj("Pa", i, last, flat(PcT[1], 0), flat(PcT[0], 0))
                if not last:
                    cT_(1, i)
                if not first:
                    statistics(2, i - 1, 1 - par)
                pj("Pb", i, last, flat(PcT[1], 1), flat(PcT[0], 1))
                for r in range(4):
                    if not last:
                        xT_(r, i)
                    x1(r, i, last, par)
                    if r == 1 and not first:
                        statistics(3, i - 1, 1 - par)
                yT_(0, 0, i, last)
                yT_(0, 1, i, last)
                if not first:
                    variances(i - 1)
                if not last:
                    u_(0, i)
                yT_(1, 0, i, last)
                maxima(1, 0, i, last)
                w_inv(0, i, last)
                yT_(1, 1, i, last)
                w_(0, i)
                if not last:
                    u_(1, i)
                maxima(1, 1, i, last)
                w_inv(1, i, last)
                pj("wa", i, last, flat(wcT[1], 0), flat(wcT[0], 0))
                if not last:
                    maxima(0, 0, i, last)
                w_(1, i)
                if not last:
                    maxima(0, 1, i, last)
                    G_(0, i, last)
                s_(0, i, last)
                pj("wb", i, last, flat(wcT[1], 1), flat(wcT[0], 1))
                s_(1, i, last)
                if not last:
                    G_(1, i, last)
                for r in range(4):
                    x2(r, i, last, par)

            body(0, 0, False, True)
            body(1, 1, False)
            with dve.Fori(1, PAIRS // 2 - 1) as j:
                body(2 * j, 0, False)
                body(2 * j + 1, 1, False)
            body(PAIRS - 2, 0, False)
            body(PAIRS - 1, 1, True)
            for r in range(4):
                statistics(r, PAIRS - 1, 1)
            variances(PAIRS - 1)

        @block.gpsimd
        def _(pool):
            nc.gpsimd.memset(ident[:, :], 0.0).then_inc(const_set, 1)
            pool.wait_ge(const_set, 1)
            nc.gpsimd.affine_select(out=ident[:, :], in_=ident[:, :], compare_op=ALU.not_equal, fill=1.0,
                                    base=0, pattern=[[-1, P]], channel_multiplier=1).then_inc(const_set, 1)

            def context(i, par):
                pool.wait_ge(Cs_hi, i + 1)
                nc.gpsimd.tensor_tensor(Cs[par][1][:, :, :], C[:, :, :], fp(Cs[par][0][:, :, :]),
                                        ALU.subtract).then_inc(Cs_set, 1)

            def residual(i, par, first=False):
                pool.wait_ge(tp_full, TP.number("xT3", None if first else i - 1) + 1)
                if not (isinstance(i, int) and i < 2):
                    pool.wait_ge(Y_set, 4 * i - 4)
                for r in range(4):
                    done = nc.gpsimd.tensor_tensor(R[par][:, r, :], X[:, r, :], c1_b[:, :], ALU.add)
                done.then_inc(R_set, 1)

            def scales(i):
                pool.wait_ge(mv_set, i + 1)
                nc.gpsimd.tensor_tensor(rstd[:, :], ve[:, :], half[:, :], ALU.pow).then_inc(norm_step, 1)
                pool.wait_ge(norm_step, i + 1)
                nc.gpsimd.tensor_tensor(nmr[:, :], nmu[:, :], rstd[:, :], ALU.mult).then_inc(norm_set, 1)

            def finish(i):
                for r in range(5):
                    if r < 4:
                        pool.wait_ge(Y_set, 4 * i + (r + 1))
                        nc.gpsimd.tensor_tensor(Y[:, r, :], Y[:, r, :], gamma_b[:, :], ALU.mult
                                                ).then_inc(Y_mul, 1)
                    if r > 0:
                        pool.wait_ge(Y_mul, 4 * i + r)
                        done = nc.gpsimd.tensor_tensor(Y[:, r - 1, :], Y[:, r - 1, :], beta_b[:, :], ALU.add)
                done.then_inc(Y_done, 1)

            def body(i, par, first=False):
                context(i + 1, 1 - par)
                if not first:
                    scales(i - 1)
                residual(i + 1, 1 - par)
                if not first:
                    finish(i - 1)

            context(0, 0)
            pool.wait_ge(su_dve, 10)
            residual(0, 0, True)
            body(0, 0, True)
            body(1, 1)
            with pool.Fori(1, PAIRS // 2 - 1) as j:
                body(2 * j, 0)
                body(2 * j + 1, 1)
            body(PAIRS - 2, 0)
            for i in (PAIRS - 2, PAIRS - 1):
                scales(i)
                finish(i)


_INS = ["x", "ctx_512", "L0_xattn_Wq", "L0_xattn_bq", "L0_xattn_Wk", "L0_xattn_Wv", "L0_xattn_bv",
        "L0_xattn_Wo", "L0_xattn_bo", "L1_xattn_Wq", "L1_xattn_Wk", "L1_xattn_bk", "L1_xattn_Wv",
        "L1_xattn_bv", "L1_xattn_gamma", "L1_xattn_beta"]


def kernel(**inputs):
    import numpy as _np
    import concourse.bacc as _bacc
    from concourse import mybir as _mybir
    from concourse.bass_utils import run_bass_kernel_spmd as _run

    nc = _bacc.Bacc("TRN2", target_bir_lowering=False, num_devices=1)
    arrays, args = {}, []
    for name in _INS:
        a = _np.ascontiguousarray(inputs[name])
        arrays[f"in_{name}"] = a
        args.append(nc.dram_tensor(f"in_{name}", a.shape, _mybir.dt.from_np(a.dtype), kind="ExternalInput").ap())
    args.append(nc.dram_tensor("out", (NSEQ, S, D), _mybir.dt.float32, kind="ExternalOutput").ap())
    build(nc, *args)
    r = _run(nc, [arrays], core_ids=[0])
    return r.results[0]["out"]
```

```python
import concourse.bass as bass
from concourse import mybir
from contextlib import ExitStack

P = 128
NSEQ, S, D, L = 64, 256, 512, 256
H = 512
PAIRS = NSEQ // 2
DT, LT, HT, ST = D // P, L // P, H // P, S // P
W = 2 * S
SCALE = float(H) ** -0.5
EPS = 1e-6

TP_BODY = ["cT0", "cT1", "xT0", "xT1", "xT2", "xT3", "yTa0", "yTa1", "yTb0", "ga", "yTb1", "gb",
           "sa", "PTa", "sb", "PTb"]
PJ_BODY = ["Pa", "Pb", "u0", "va", "u1", "vb", "wa", "wb"]
OT_BODY = ["out0", "out1", "out2", "out3", "pred0", "pred1", "pred2", "pred3"]
TP_FRONT = ["cT0", "cT1", "xT0", "xT1", "xT2", "xT3", "PTa", "PTb"]
PJ_FRONT = ["u0", "u1"]


class Ring:

    def __init__(self, front, body):
        self.front, self.body = front, body
        self.last = [n for n in body if n not in front]

    def index(self, name, i, last):
        if i is None:
            return self.front.index(name)
        return (self.last if last else self.body).index(name)

    def number(self, name, i, last=False):
        if i is None:
            return self.index(name, i, last)
        return i * len(self.body) + (len(self.front) + self.index(name, i, last))

    def bank(self, name, i, last=False):
        return self.index(name, i, last) % 2


TP, PJ, OT = Ring(TP_FRONT, TP_BODY), Ring(PJ_FRONT, PJ_BODY), Ring([], OT_BODY)


def following(i):
    return 0 if i is None else i + 1


def build(nc, x, ctxt, Wq0, bq0, Wk0, Wv0, bv0, Wo0, bo0, Wq1, Wk1, bk1, Wv1, bv1, gamma, beta, out):
    f32, f32r = mybir.dt.float32, mybir.dt.float32r
    ALU, ACT, AX = mybir.AluOpType, mybir.ActivationFunctionType, mybir.AxisListType

    x_v = x.rearrange("(n s) (p q) d -> n p s (q d)", s=2, q=ST)
    c_v = ctxt.rearrange("(n s) (p q) d -> n p s (q d)", s=2, q=ST)
    o_v = out.rearrange("(n s) (p q) d -> n p s (q d)", s=2, q=ST)

    with ExitStack() as stack:
        def sb(name, shape, dt=f32):
            return stack.enter_context(nc.sbuf_tensor(name, shape, dt))

        def split(name, shape):
            return [sb(name + "_hi", shape, f32r), sb(name + "_lo", shape, f32r)]

        def sem(name):
            return stack.enter_context(nc.semaphore(name))

        ident = sb("ident", [P, P])
        A0 = split("A0", [P, DT, L])
        Bv = split("Bv", [P, LT, D])
        A1 = split("A1", [P, DT, L])
        V1 = split("V1", [P, LT, D])
        pick = sb("pick", [P, P], f32r)
        pick_f = sb("pick_f", [P, P])
        ones_f = sb("ones_f", [P, P])
        bvK = sb("bvK", [P, D], f32r)
        c0 = sb("c0", [P, LT])
        g1_b = sb("g1_b", [P, D])
        c1_b = sb("c1_b", [P, D])
        gamma_b = sb("gamma_b", [P, D])
        beta_b = sb("beta_b", [P, D])
        bcol = sb("bcol", [P, 3, HT])
        half = sb("half", [P, 2 * ST])

        with ExitStack() as scratch:
            def early(name, shape):
                return scratch.enter_context(nc.sbuf_tensor(name, shape, f32))[:, :, :]

            WkN = early("WkN", [P, LT, H])
            WkT = early("WkT", [P, HT, L])
            WvN = early("WvN", [P, LT, H])
            WvT = early("WvT", [P, HT, L])
            bvw = early("bvw", [P, HT, P])
            bkw = early("bkw", [P, HT, P])
        yT = split("yT", [P, 2, DT, S])
        PcT = split("PcT", [P, 2, LT, S])

        X = sb("X", [P, 2 * ST, D])
        R = [sb(f"R{n}", [P, 2 * ST, D]) for n in range(2)]
        Y = sb("Y", [P, 2 * ST, D])
        C = sb("C", [P, 2 * ST, L])
        Cs = [split(f"C{n}", [P, 2 * ST, L]) for n in range(2)]
        cTs = [split(f"cT{n}", [P, LT, W]) for n in range(2)]
        xT = split("xT", [P, DT, W])
        uT = split("uT", [P, LT, W])
        vT = split("vT", [P, 2, LT, S])
        gx = sb("gx", [P, D])
        gcol = sb("gcol", [P, 4])
        gT = sb("gT", [P, 2, S])
        E0 = sb("E0", [P, 2 * ST, S])
        PT = split("PT", [P, 2, ST, S])
        E1 = sb("E1", [P, 2 * ST, S])
        w = split("w", [P, 2, ST, S])
        wcT = split("wcT", [P, 2, LT, S])
        srow = sb("srow", [P, 2, S], f32r)
        nmax0, Z0, rz0 = sb("nmax0", [P, 4]), sb("Z0", [P, 4]), sb("rz0", [P, 4])
        nmax1, Z1, rz1 = sb("nmax1", [P, 4]), sb("Z1", [P, 4]), sb("rz1", [P, 4])
        stats = sb("stats", [P, 4, 6])
        msum = sb("msum", [P, 4, 2])
        mdif, msq, vin = (sb(n, [P, 4]) for n in ("mdif", "msq", "vin"))
        ve, rstd, nmu, nmr = (sb(n, [P, 4]) for n in ("ve", "rstd", "nmu", "nmr"))

        bank = [stack.enter_context(nc.psum_tensor(f"bank{n}", [P, 512], f32)) for n in range(8)]
        tp_bank, pj_bank, ot_bank = bank[0:2], bank[2:4], bank[6:8]
        S0_bank, S1_bank = bank[4], bank[5]

        w_in = [sem(f"w_in{n}") for n in range(7)]
        b_in = sem("b_in")
        const_set = sem("const_set")
        su_full = sem("su_full")
        su_act, su_dve = sem("su_act"), sem("su_dve")
        x_in, c_in, y_out = sem("x_in"), sem("c_in"), sem("y_out")
        tp_full, tp_hi, tp_free = sem("tp_full"), sem("tp_hi"), sem("tp_free")
        pj_full, pj_hi, pj_free = sem("pj_full"), sem("pj_hi"), sem("pj_free")
        ot_full, ot_free = sem("ot_full"), sem("ot_free")
        S0_full, neg_max0, E0_set = sem("S0_full"), sem("neg_max0"), sem("E0_set")
        S1_full, neg_max1, E1_set = sem("S1_full"), sem("neg_max1"), sem("E1_set")
        S1_sum = sem("S1_sum")
        g_set = sem("g_set")
        rz1_set = sem("rz1_set")
        w_hi, w_lo = sem("w_hi"), sem("w_lo")
        Cs_set = sem("Cs_set")
        R_set = sem("R_set")
        mv_set = sem("mv_set")
        norm_set = sem("norm_set")
        Y_set = sem("Y_set")
        Y_mul = sem("Y_mul")
        Y_done = sem("Y_done")
        tail_step = sem("tail_step")
        tail_done = sem("tail_done")
        Cs_hi = sem("Cs_hi")
        norm_step = sem("norm_step")
        rz0_set = sem("rz0_set")
        ln_step = sem("ln_step")

        def fp(ap):
            return ap.bitcast(f32)

        WqN = R[0][:, :, :]
        WqT = R[1][:, :, :]
        WoN = Y[:, :, :]
        bv1_b = gx

        block = stack.enter_context(nc.Block())

        @block.sync
        def _(sp):
            def rows(a):
                return a.rearrange("(t p) n -> p t n", p=P)

            sp.dma_start(WkN, rows(Wk0)).then_inc(w_in[1], 16)
            sp.dma_start(WqN, rows(Wq0)).then_inc(w_in[0], 16)
            sp.dma_start(WvN, rows(Wv0)).then_inc(w_in[2], 16)
            def load_C(n):
                sp.dma_start(C[:, :, :].rearrange("p (s q) l -> p s (q l)", s=2), c_v[n]).then_inc(c_in, 16)

            def load_X(n):
                sp.dma_start(X[:, :, :].rearrange("p (s q) d -> p s (q d)", s=2), x_v[n]).then_inc(x_in, 16)

            load_C(0)
            sp.dma_start(WoN, Wo0.rearrange("(p t) n -> p t n", p=P)).then_inc(w_in[3], 16)
            load_X(0)
            sp.wait_ge(su_full, 6)
            sp.dma_start(WqN, rows(Wq1)).then_inc(w_in[4], 16)
            sp.dma_start(WkN, rows(Wk1)).then_inc(w_in[5], 16)
            sp.wait_ge(su_full, 8)
            sp.dma_start(WvN, rows(Wv1)).then_inc(w_in[6], 16)

            def load(n):
                first = isinstance(n, int) and n == 1
                sp.wait_ge(tp_full, TP.number("cT1", None if first else n - 2) + 1)
                sp.wait_ge(Cs_set, n)
                load_C(n)
                sp.wait_ge(R_set, n)
                load_X(n)

            def store(i):
                sp.wait_ge(Y_done, i + 1)
                sp.dma_start(o_v[i], Y[:, :, :].rearrange("p (s q) d -> p s (q d)", s=2)).then_inc(y_out, 16)

            load(1)
            load(2)
            with sp.Fori(3, PAIRS) as n:
                load(n)
                store(n - 3)
            store(PAIRS - 3)
            store(PAIRS - 2)
            for s in range(2):
                sp.wait_ge(tail_done, 2 + s)
                if s == 1:
                    sp.wait_ge(Y_done, PAIRS)
                sp.dma_start(o_v[PAIRS - 1][:, s, :], Y[:, 2 * s:2 * s + 2, :].rearrange("p q d -> p (q d)")
                             ).then_inc(y_out, 16)
            sp.wait_ge(y_out, 16 * (PAIRS + 1))

        @block.tensor
        def _(pe):
            def product(dst, stat, mov, k, first=True):
                for t in range(k):
                    for n, (a, b) in enumerate(((0, 0), (0, 1), (1, 0))):
                        last = nc.tensor.matmul(dst, stat(a, t), mov(b, t), start=(first and t == 0 and n == 0),
                                                stop=(t == k - 1 and n == 2))
                return last

            def transposes(dst, src):
                for n, s in enumerate(src):
                    last = nc.tensor.transpose(dst[:, n * P:(n + 1) * P], s, ident[:, :])
                return last

            def transposed_Wq(bank_of):
                for h in range(HT):
                    transposes(bank[bank_of[h]], [WqN[:, d, h::HT] for d in range(DT)]).then_inc(su_full, 1)

            def transposed_256(src, bank_of):
                for h in range(0, HT, 2):
                    transposes(bank[bank_of[h // 2]], [src[:, l, k::HT] for k in (h, h + 1)
                                                       for l in range(LT)]).then_inc(su_full, 1)

            def A_half(dst, n):
                for k in (0, 1):
                    d = 2 * n + k
                    for h in range(HT):
                        last = nc.tensor.matmul(dst[:, k * L:(k + 1) * L], WqT[:, h, d * P:(d + 1) * P],
                                                WkT[:, h, :], start=(h == 0), stop=(h == HT - 1))
                last.then_inc(su_full, 1)

            def over_h(dst, stat, mov):
                for h in range(HT):
                    last = nc.tensor.matmul(dst, stat(h), mov[:, h, :], start=(h == 0), stop=(h == HT - 1))
                last.then_inc(su_full, 1)

            def take(ring, name, i, last, free):
                k = ring.number(name, i, last)
                if not (isinstance(k, int) and k < 2):
                    pe.wait_ge(free, k - 1)

            def tp(name, i, last, src):
                take(TP, name, i, last, tp_free)
                transposes(tp_bank[TP.bank(name, i, last)], src).then_inc(tp_full, 1)

            def tp_ready(name, i, last):
                pe.wait_ge(tp_free, TP.number(name, i, last) + 1)

            def pj_ready(name, i, last):
                pe.wait_ge(pj_free, PJ.number(name, i, last) + 1)

            def cT_(l, i):
                tp(f"cT{l}", i, False, [C[:, r, l * P:(l + 1) * P] for r in range(4)])

            def xT_(d, i):
                tp(f"xT{d}", i, False, [X[:, r, d * P:(d + 1) * P] for r in range(4)])

            def u_(l, i):
                take(PJ, f"u{l}", i, False, pj_free)
                product(pj_bank[PJ.bank(f"u{l}", i)][:, :], lambda a, t: A0[a][:, t, l * P:(l + 1) * P],
                        lambda b, t: xT[b][:, t, :], DT).then_inc(pj_full, 1)

            def S0_(s, i, par):
                if i is not None or s > 0:
                    pe.wait_ge(E0_set, 2 * following(i) + s)
                for q in range(ST):
                    r = s * S + q * P
                    last = product(S0_bank[:, q * S:(q + 1) * S],
                                   lambda a, t: uT[a][:, t, r:r + P],
                                   lambda b, t: cTs[par][b][:, t, s * S:(s + 1) * S], LT)
                last.then_inc(S0_full, 1)

            def PT_(s, i):
                pe.wait_ge(E0_set, 2 * following(i) + (s + 1))
                tp("PT" + "ab"[s], i, False,
                   [E0[:, 2 * s + q, k * P:(k + 1) * P] for k in range(ST) for q in range(ST)])

            def Pc_(s, i, last, par):
                name = "P" + "ab"[s]
                tp_ready("PT" + "ab"[s], None if isinstance(i, int) and i == 0 else i - 1, False)
                if s == 0:
                    pe.wait_ge(Cs_set, i + 1)
                take(PJ, name, i, last, pj_free)
                for l in range(LT):
                    done = product(pj_bank[PJ.bank(name, i, last)][:, l * S:(l + 1) * S],
                                   lambda a, t: Cs[par][a][:, 2 * s + t, l * P:(l + 1) * P],
                                   lambda b, t: PT[b][:, s, t, :], ST)
                done.then_inc(pj_full, 1)

            def out_(r, i, last):
                s, q = divmod(r, ST)
                if q == 0:
                    pj_ready("P" + "ab"[s], i, last)
                take(OT, f"out{r}", i, last, ot_free)
                product(ot_bank[OT.bank(f"out{r}", i)][:, :], lambda a, t: PcT[a][:, s, t, q * P:(q + 1) * P],
                        lambda b, t: Bv[b][:, t, :], LT).then_inc(ot_full, 1)

            def yT_(s, n, i, last, par):
                pe.wait_ge(ot_free, OT.number(f"out{2 * s + 1}", i, last) + 1)
                tp(f"yT{'ab'[s]}{n}", i, last, [R[par][:, 2 * s + q, d * P:(d + 1) * P]
                                                for d in (2 * n, 2 * n + 1) for q in range(ST)])

            def g_(s, i, last):
                pe.wait_ge(g_set, 4 * i + (2 * s + 2))
                tp("g" + "ab"[s], i, last, [gcol[:, r:r + 1].to_broadcast([P, P]) for r in (2 * s, 2 * s + 1)])

            def v_(s, i, last):
                name = "v" + "ab"[s]
                tp_ready(f"yT{'ab'[s]}1", i, last)
                take(PJ, name, i, last, pj_free)
                for l in range(LT):
                    done = product(pj_bank[PJ.bank(name, i, last)][:, l * S:(l + 1) * S],
                                   lambda a, t: A1[a][:, t, l * P:(l + 1) * P],
                                   lambda b, t: yT[b][:, s, t, :], DT)
                done.then_inc(pj_full, 1)

            def S1_(s, i, last, par):
                pj_ready("v" + "ab"[s], i, last)
                if not (isinstance(i, int) and i == 0 and s == 0):
                    pe.wait_ge(S1_sum, 2 * i + s)
                for m in range(ST):
                    c = s * S + m * P
                    done = product(S1_bank[:, m * S:(m + 1) * S],
                                   lambda a, t: cTs[par][a][:, t, c:c + P],
                                   lambda b, t: vT[b][:, s, t, :], LT)
                done.then_inc(S1_full, 1)

            def wc_(s, i, last, par):
                name = "w" + "ab"[s]
                take(PJ, name, i, last, pj_free)
                for l in range(LT):
                    done = product(pj_bank[PJ.bank(name, i, last)][:, l * S:(l + 1) * S],
                                   lambda a, t: Cs[par][a][:, 2 * s + t, l * P:(l + 1) * P],
                                   lambda b, t: w[b][:, s, t, :], ST)
                done.then_inc(pj_full, 1)

            def s_(s, i, last):
                name = "s" + "ab"[s]
                pe.wait_ge(w_lo, 2 * i + (s + 1))
                take(TP, name, i, last, tp_free)
                dst = tp_bank[TP.bank(name, i, last)][:, 0:S]
                for t in range(ST):
                    for b in range(2):
                        done = nc.tensor.matmul(dst, pick[:, :], w[b][:, s, t, :], start=(t == 0 and b == 0),
                                                stop=(t == ST - 1 and b == 1))
                done.then_inc(tp_full, 1)

            def pred_(r, i, last):
                s, q = divmod(r, ST)
                if q == 0:
                    pj_ready("w" + "ab"[s], i, last)
                    tp_ready("s" + "ab"[s], i, last)
                take(OT, f"pred{r}", i, last, ot_free)
                dst = ot_bank[OT.bank(f"pred{r}", i)][:, :]
                nc.tensor.matmul(dst, srow[:, s, q * P:(q + 1) * P], bvK[:, :], start=True, stop=False)
                product(dst, lambda a, t: wcT[a][:, s, t, q * P:(q + 1) * P],
                        lambda b, t: V1[b][:, t, :], LT, first=False).then_inc(ot_full, 1)

            pe.wait_ge(const_set, 2)
            pe.wait_ge(w_in[1], 16)
            transposed_256(WkN, (4, 5))
            pe.wait_ge(w_in[0], 16)
            transposed_Wq((0, 1, 2, 3))
            pe.wait_ge(w_in[2], 16)
            transposed_256(WvN, (6, 7))
            pe.wait_ge(su_act, 4)
            pe.wait_ge(su_dve, 3)
            A_half(bank[0], 0)
            A_half(bank[1], 1)
            pe.wait_ge(b_in, 7 * 16)
            for l in range(LT):
                for h in range(HT):
                    last = nc.tensor.matmul(bank[2][:, l:l + 1], WkT[:, h, l * P:(l + 1) * P],
                                            bcol[:, 0, h:h + 1], start=(h == 0), stop=(h == HT - 1))
            last.then_inc(su_full, 1)
            pe.wait_ge(su_dve, 5)
            pe.wait_ge(w_in[3], 16)
            over_h(bank[6][:, :], lambda h: WvT[:, h, 0:P], WoN)
            pe.wait_ge(su_dve, 7)
            pe.wait_ge(c_in, 16)
            cT_(0, None)
            cT_(1, None)
            over_h(bank[7][:, :], lambda h: WvT[:, h, P:2 * P], WoN)
            pe.wait_ge(x_in, 16)
            xT_(0, None)
            xT_(1, None)
            over_h(bank[5][:, :], lambda h: bvw[:, h, :], WoN)
            xT_(2, None)
            xT_(3, None)
            pe.wait_ge(su_dve, 10)
            pe.wait_ge(w_in[4], 16)
            transposed_Wq((2, 3, 6, 7))
            pe.wait_ge(su_dve, 11)
            pe.wait_ge(w_in[5], 16)
            transposed_256(WkN, (4, 5))
            tp_ready("xT3", None, False)
            pe.wait_ge(su_act, 12)
            u_(0, None)
            u_(1, None)
            pe.wait_ge(su_dve, 13)
            A_half(bank[6], 0)
            pj_ready("u1", None, False)
            S0_(0, None, 0)
            A_half(bank[7], 1)
            S0_(1, None, 0)
            PT_(0, None)
            over_h(bank[5][:, :], lambda h: bkw[:, h, :], WqT)
            PT_(1, None)
            pe.wait_ge(su_dve, 18)

            def body(i, par, last):
                Pc_(0, i, last, par)
                if not last:
                    pe.wait_ge(c_in, 16 * i + 32)
                    cT_(0, i)
                Pc_(1, i, last, par)
                if not last:
                    cT_(1, i)
                    pe.wait_ge(x_in, 16 * i + 32)
                for r in range(4):
                    if not last:
                        xT_(r, i)
                    out_(r, i, last)
                yT_(0, 0, i, last, par)
                yT_(0, 1, i, last, par)
                if not last:
                    tp_ready("xT3", i, last)
                    u_(0, i)
                yT_(1, 0, i, last, par)
                v_(0, i, last)
                g_(0, i, last)
                yT_(1, 1, i, last, par)
                if not last:
                    u_(1, i)
                S1_(0, i, last, par)
                v_(1, i, last)
                g_(1, i, last)
                if not last:
                    pj_ready("u1", i, last)
                    S0_(0, i, 1 - par)
                S1_(1, i, last, par)
                s_(0, i, last)
                wc_(0, i, last, par)
                if not last:
                    S0_(1, i, 1 - par)
                    PT_(0, i)
                pred_(0, i, last)
                s_(1, i, last)
                wc_(1, i, last, par)
                pred_(1, i, last)
                if not last:
                    PT_(1, i)
                pred_(2, i, last)
                pred_(3, i, last)

            body(0, 0, False)
            body(1, 1, False)
            with pe.Fori(1, PAIRS // 2 - 1) as j:
                body(2 * j, 0, False)
                body(2 * j + 1, 1, False)
            body(PAIRS - 2, 0, False)
            body(PAIRS - 1, 1, True)

        @block.scalar
        def _(act):
            def copy(dst, src, **kw):
                return nc.scalar.activation(dst, src, ACT.Copy, **kw)

            for n, v in enumerate((bq0, bv0, bk1)):
                act.dma_start(bcol[:, n, :], v.rearrange("(p t) -> p t", p=P)).then_inc(b_in, 16)
            for dst, v in ((c1_b, bo0), (bv1_b, bv1), (gamma_b, gamma), (beta_b, beta)):
                act.dma_start(dst[:, :], v.rearrange("(a n) -> a n", a=1).to_broadcast([P, D])
                              ).then_inc(b_in, 16)
            def tp(name, i, last, dst, cols=slice(0, 512)):
                k = TP.number(name, i, last)
                act.wait_ge(tp_full, k + 1)
                copy(dst, tp_bank[TP.bank(name, i, last)][:, cols]).then_inc(tp_hi, 1)

            def pj(name, i, last, dst, bias=None):
                k = PJ.number(name, i, last)
                act.wait_ge(pj_full, k + 1)
                src = pj_bank[PJ.bank(name, i, last)][:, :]
                if bias is None:
                    copy(dst, src).then_inc(pj_hi, 1)
                else:
                    nc.scalar.activation(dst, src, ACT.Identity, bias=bias).then_inc(pj_hi, 1)

            def exps0(s, i):
                act.wait_ge(neg_max0, 2 * following(i) + (s + 1))
                for q in range(ST):
                    r = 2 * s + q
                    done = nc.scalar.activation(E0[:, r, :], S0_bank[:, q * S:(q + 1) * S],
                                                ACT.Exp, bias=nmax0[:, r:r + 1], accum_out=Z0[:, r:r + 1])
                done.then_inc(E0_set, 1)

            def exps1(s, i):
                act.wait_ge(neg_max1, 2 * i + (s + 1))
                for m in range(ST):
                    r = 2 * s + m
                    done = nc.scalar.activation(E1[:, r, :], E1[:, r, :],
                                                ACT.Exp, bias=nmax1[:, r:r + 1], accum_out=Z1[:, r:r + 1])
                done.then_inc(E1_set, 1)

            def w_(s, i):
                act.wait_ge(rz1_set, 2 * i + (s + 1))
                for m in range(ST):
                    r = 2 * s + m
                    done = copy(w[0][:, s, m, :], E1[:, r, :], scale=rz1[:, r:r + 1])
                    done.then_inc(w_hi, 1)

            def s_(s, i, last):
                tp("s" + "ab"[s], i, last, srow[:, s, :], slice(0, S))

            def normalise(r, i, par):
                if r == 0:
                    act.wait_ge(norm_set, i + 1)
                    if not (isinstance(i, int) and i == 0):
                        act.wait_ge(y_out, 16 * i)
                nc.scalar.activation(Y[:, r, :], R[par][:, r, :], ACT.Identity, bias=nmr[:, r:r + 1],
                                     scale=rstd[:, r:r + 1]).then_inc(Y_set, 1)

            def context(i, par):
                act.wait_ge(c_in, 16 * i + 16)
                if not (isinstance(i, int) and i < 2):
                    act.wait_ge(pj_full, PJ.number("wb", i - 2) + 1)
                copy(Cs[par][0][:, :, :], C[:, :, :]).then_inc(Cs_hi, 1)

            def cT_(l, i, par):
                tp(f"cT{l}", i, False, cTs[par][0][:, l, :])

            def xT_(d, i):
                tp(f"xT{d}", i, False, xT[0][:, d, :])

            def u_(l, i):
                pj(f"u{l}", i, False, uT[0][:, l, :], c0[:, l:l + 1])

            def v_(s, i, last):
                pj("v" + "ab"[s], i, last, flat(vT[0], s))

            def g_(s, i, last):
                tp("g" + "ab"[s], i, last, gT[:, s, 0:P], slice(0, P))

            def flat(t, s):
                return t[:, s, :, :].rearrange("p a b -> p (a b)")

            def yT_(s, n, i, last):
                tp(f"yT{'ab'[s]}{n}", i, last, yT[0][:, s, 2 * n:2 * n + 2, :].rearrange("p a b -> p (a b)"))

            def WqT_(first, h):
                act.wait_ge(su_full, first + h)
                src = bank[(h if first == 3 else (2, 3, 6, 7)[h])]
                copy(WqT[:, h, :], src[:, :]).then_inc(su_act, 1)

            def A_hi(dst, n, src, full):
                act.wait_ge(su_full, full)
                copy(dst[:, 2 * n:2 * n + 2, :], src[:, :].rearrange("p (a b) -> p a b", a=2),
                     scale=SCALE).then_inc(su_act, 1)

            for h in range(HT):
                WqT_(3, h)
            A_hi(A0[0], 0, bank[0], 9)
            A_hi(A0[0], 1, bank[1], 10)
            context(0, 0)
            act.wait_ge(su_full, 12)
            copy(Bv[0][:, 0, :], bank[6][:, :]).then_inc(su_act, 1)
            cT_(0, None, 0)
            cT_(1, None, 0)
            act.wait_ge(su_full, 13)
            copy(Bv[0][:, 1, :], bank[7][:, :]).then_inc(su_act, 1)
            for d in range(DT):
                xT_(d, None)
            for h in range(HT):
                WqT_(15, h)
            act.wait_ge(w_in[6], 16)
            copy(V1[0][:, :, :], WvN).then_inc(su_act, 1)
            act.wait_ge(b_in, 7 * 16)
            for r in (0, 32):
                copy(bvK[r:r + 1, :], bv1_b[r:r + 1, :])
            copy(w[0][64:65, :, :, :].rearrange("p a b c -> p (a b c)")[:, 0:D], bv1_b[64:65, :]
                 ).then_inc(su_act, 1)
            act.wait_ge(su_dve, 8)
            u_(0, None)
            u_(1, None)
            A_hi(A1[0], 0, bank[6], 21)
            exps0(0, None)
            A_hi(A1[0], 1, bank[7], 22)
            exps0(1, None)
            tp("PTa", None, False, flat(PT[0], 0))
            tp("PTb", None, False, flat(PT[0], 1))
            act.wait_ge(su_dve, 18)

            def body(i, par, last, first=False):
                pj("Pa", i, last, flat(PcT[0], 0))
                if not last:
                    cT_(0, i, 1 - par)
                pj("Pb", i, last, flat(PcT[0], 1))
                if not last:
                    cT_(1, i, 1 - par)
                    context(i + 1, 1 - par)
                for r in range(4):
                    if not last:
                        xT_(r, i)
                    if r > 0 and not first:
                        normalise(r - 1, i - 1, 1 - par)
                yT_(0, 0, i, last)
                if not first:
                    normalise(3, i - 1, 1 - par)
                yT_(0, 1, i, last)
                if not last:
                    u_(0, i)
                yT_(1, 0, i, last)
                v_(0, i, last)
                g_(0, i, last)
                yT_(1, 1, i, last)
                if not last:
                    u_(1, i)
                exps1(0, i)
                v_(1, i, last)
                w_(0, i)
                g_(1, i, last)
                if not last:
                    exps0(0, i)
                s_(0, i, last)
                exps1(1, i)
                w_(1, i)
                if not last:
                    tp("PTa", i, last, flat(PT[0], 0))
                    exps0(1, i)
                s_(1, i, last)
                pj("wb", i, last, flat(wcT[0], 1))
                if not last:
                    tp("PTb", i, last, flat(PT[0], 1))

            body(0, 0, False, True)
            body(1, 1, False)
            with act.Fori(1, PAIRS // 2 - 1) as j:
                body(2 * j, 0, False)
                body(2 * j + 1, 1, False)
            body(PAIRS - 2, 0, False)
            body(PAIRS - 1, 1, True)
            act.wait_ge(norm_set, PAIRS)
            act.wait_ge(y_out, 16 * (PAIRS - 1))
            normalise(3, PAIRS - 1, 1)

        @block.vector
        def _(dve):
            def minus(dst, src, hi):
                return nc.vector.tensor_tensor(dst, src, fp(hi), ALU.subtract)

            nc.vector.memset(half[:, :], -0.5)
            for c in (0, 32, 64):
                nc.vector.memset(pick_f[:, c:c + 1], 1.0)
                nc.vector.memset(pick_f[:, c + 1:c + 32 if c < 64 else P], 0.0)
            nc.vector.memset(fp(bvK[:, :]), 0.0)
            nc.vector.memset(ones_f[:, :], 1.0).then_inc(su_dve, 1)
            def tp(name, i, last, dst, hi):
                dve.wait_ge(tp_hi, TP.number(name, i, last) + 1)
                minus(dst, tp_bank[TP.bank(name, i, last)][:, :], hi).then_inc(tp_free, 1)

            def pj(name, i, last, dst, hi, bias=None):
                dve.wait_ge(pj_hi, PJ.number(name, i, last) + 1)
                src = pj_bank[PJ.bank(name, i, last)][:, :]
                if bias is None:
                    minus(dst, src, hi).then_inc(pj_free, 1)
                else:
                    nc.vector.scalar_tensor_tensor(dst, src, bias, fp(hi), ALU.add, ALU.subtract
                                                   ).then_inc(pj_free, 1)

            def negated_maxima(dst, s, src):
                return nc.vector.tensor_reduce(dst[:, 2 * s:2 * s + 2], src, AX.X, ALU.max, negate=True)

            def maxima0(s, i):
                dve.wait_ge(S0_full, 2 * following(i) + (s + 1))
                negated_maxima(nmax0, s, S0_bank[:, :].rearrange("p (a b) -> p a b", a=ST)
                               ).then_inc(neg_max0, 1)

            def maxima1(s, i, last):
                dve.wait_ge(tp_free, TP.number("g" + "ab"[s], i, last) + 1)
                dve.wait_ge(S1_full, 2 * i + (s + 1))
                nc.vector.tensor_tensor(E1[:, 2 * s:2 * s + 2, :],
                                        S1_bank[:, :].rearrange("p (a b) -> p a b", a=ST),
                                        gT[:, s:s + 1, :].to_broadcast([P, ST, S]), ALU.add).then_inc(S1_sum, 1)
                dve.wait_ge(S1_sum, 2 * i + (s + 1))
                negated_maxima(nmax1, s, E1[:, 2 * s:2 * s + 2, :]).then_inc(neg_max1, 1)

            def cT_(l, i, par):
                tp(f"cT{l}", i, False, cTs[par][1][:, l, :], cTs[par][0][:, l, :])

            def xT_(d, i):
                tp(f"xT{d}", i, False, xT[1][:, d, :], xT[0][:, d, :])

            def u_(l, i):
                pj(f"u{l}", i, False, uT[1][:, l, :], uT[0][:, l, :], c0[:, l:l + 1])

            def v_(s, i, last):
                pj("v" + "ab"[s], i, last, flat(vT[1], s), flat(vT[0], s))

            def g_(s, i, last):
                name = "g" + "ab"[s]
                dve.wait_ge(tp_hi, TP.number(name, i, last) + 1)
                nc.vector.tensor_copy(gT[:, s, P:S], tp_bank[TP.bank(name, i, last)][:, P:S]
                                      ).then_inc(tp_free, 1)

            def flat(t, s):
                return t[:, s, :, :].rearrange("p a b -> p (a b)")

            def s_(s, i, last):
                name = "s" + "ab"[s]
                dve.wait_ge(tp_hi, TP.number(name, i, last) + 1)
                minus(srow[32:33, s, :], tp_bank[TP.bank(name, i, last)][32:33, 0:S], srow[32:33, s, :]
                      ).then_inc(tp_free, 1)

            def yT_(s, n, i, last):
                tp(f"yT{'ab'[s]}{n}", i, last, *[yT[a][:, s, 2 * n:2 * n + 2, :].rearrange(
                    "p a b -> p (a b)") for a in (1, 0)])

            def P_inv(i):
                dve.wait_ge(E0_set, 2 * i + 2)
                nc.vector.reciprocal(rz0[:, :], Z0[:, :]).then_inc(rz0_set, 1)

            def x1(r, i, last, par):
                if r == 0:
                    dve.wait_ge(R_set, i + 1)
                    dve.wait_ge(rz0_set, i + 1)
                dve.wait_ge(ot_full, OT.number(f"out{r}", i, last) + 1)
                nc.vector.scalar_tensor_tensor(R[par][:, r, :], ot_bank[OT.bank(f"out{r}", i)][:, :],
                                               rz0[:, r:r + 1], R[par][:, r, :], ALU.mult, ALU.add
                                               ).then_inc(ot_free, 1)

            def dot(r, i, last, par):
                dve.wait_ge(ot_free, OT.number(f"out{r}", i, last) + 1)
                if not (isinstance(i, int) and i == 0 and r == 0):
                    dve.wait_ge(g_set, 4 * i + r)
                nc.vector.scalar_tensor_tensor(gx[:, :], R[par][:, r, :], 1.0, g1_b[:, :], ALU.mult, ALU.mult,
                                               accum_out=gcol[:, r:r + 1]).then_inc(g_set, 1)

            def w_inv(s, i, last):
                dve.wait_ge(E1_set, 2 * i + (s + 1))
                nc.vector.reciprocal(rz1[:, 2 * s:2 * s + 2], Z1[:, 2 * s:2 * s + 2]).then_inc(rz1_set, 1)

            def wa_hi(i, last):
                dve.wait_ge(pj_full, PJ.number("wa", i, last) + 1)
                nc.vector.tensor_copy(flat(wcT[0], 0), pj_bank[PJ.bank("wa", i, last)][:, :]).then_inc(pj_hi, 1)

            def w_(s, i):
                for m in range(ST):
                    r = 2 * s + m
                    dve.wait_ge(w_hi, 4 * i + (r + 1))
                    done = nc.vector.scalar_tensor_tensor(w[1][:, s, m, :], E1[:, r, :], rz1[:, r:r + 1],
                                                          fp(w[0][:, s, m, :]), ALU.mult, ALU.subtract)
                done.then_inc(w_lo, 1)

            def x2(r, i, last, par):
                dve.wait_ge(ot_full, OT.number(f"pred{r}", i, last) + 1)
                nc.vector.tensor_tensor(R[par][:, r, :], ot_bank[OT.bank(f"pred{r}", i)][:, :],
                                        R[par][:, r, :], ALU.add).then_inc(ot_free, 1)

            def statistics(r, i, last, par):
                dve.wait_ge(ot_free, OT.number(f"pred{r}", i, last) + 1)
                nc.vector.bn_stats(stats[:, r, :], R[par][:, r, :]).then_inc(ln_step, 1)

            def variances(i):
                dve.wait_ge(ln_step, 6 * i + 4)
                nc.vector.tensor_tensor(msum[:, :, :], stats[:, :, 1:3], stats[:, :, 4:6], ALU.add)
                nc.vector.tensor_tensor(mdif[:, :], stats[:, :, 1], stats[:, :, 4], ALU.subtract
                                        ).then_inc(ln_step, 1)
                dve.wait_ge(ln_step, 6 * i + 5)
                nc.vector.scalar_tensor_tensor(msq[:, :], mdif[:, :], 0.25, mdif[:, :], ALU.mult, ALU.mult)
                nc.vector.tensor_scalar(vin[:, :], msum[:, :, 1], 1.0 / D, EPS, ALU.mult, ALU.add
                                        ).then_inc(ln_step, 1)
                dve.wait_ge(ln_step, 6 * i + 6)
                if not (isinstance(i, int) and i == 0):
                    dve.wait_ge(norm_set, i)
                nc.vector.tensor_tensor(ve[:, :], vin[:, :], msq[:, :], ALU.add)
                nc.vector.tensor_scalar(nmu[:, :], msum[:, :, 0], -0.5, None, ALU.mult).then_inc(mv_set, 1)

            def copy_256(dst, k, src, full):
                dve.wait_ge(su_full, full)
                nc.vector.tensor_copy(dst[:, 2 * k:2 * k + 2, :], src[:, :].rearrange("p (a b) -> p a b", a=2)
                                      ).then_inc(su_dve, 1)

            def A_lo(dst, hi, n, src, step):
                dve.wait_ge(su_act, step)
                nc.vector.scalar_tensor_tensor(dst[:, 2 * n:2 * n + 2, :].rearrange("p a b -> p (a b)"),
                                               src[:, :], SCALE,
                                               fp(hi[:, 2 * n:2 * n + 2, :].rearrange("p a b -> p (a b)")),
                                               ALU.mult, ALU.subtract).then_inc(su_dve, 1)

            copy_256(WkT, 0, bank[4], 1)
            copy_256(WkT, 1, bank[5], 2)
            copy_256(WvT, 0, bank[6], 7)
            copy_256(WvT, 1, bank[7], 8)
            dve.wait_ge(b_in, 7 * 16)
            dve.wait_ge(su_dve, 1)
            nc.vector.tensor_copy(pick[:, :], pick_f[:, :])
            for h in range(HT):
                nc.vector.tensor_scalar(bvw[:, h, :], ones_f[:, :], bcol[:, 1, h:h + 1], None, ALU.mult)
                nc.vector.tensor_scalar(bkw[:, h, :], ones_f[:, :], bcol[:, 2, h:h + 1], None, ALU.mult)
            A_lo(A0[1], A0[0], 0, bank[0], 5)
            A_lo(A0[1], A0[0], 1, bank[1], 6)
            dve.wait_ge(su_full, 11)
            nc.vector.tensor_scalar(c0[:, :], bank[2][:, 0:LT], SCALE, None, ALU.mult).then_inc(su_dve, 1)
            dve.wait_ge(su_act, 7)
            minus(Bv[1][:, 0, :], bank[6][:, :], Bv[0][:, 0, :]).then_inc(su_dve, 1)
            cT_(0, None, 0)
            cT_(1, None, 0)
            dve.wait_ge(su_act, 8)
            minus(Bv[1][:, 1, :], bank[7][:, :], Bv[0][:, 1, :]).then_inc(su_dve, 1)
            xT_(0, None)
            xT_(1, None)
            dve.wait_ge(su_full, 14)
            nc.vector.tensor_tensor(c1_b[:, :], bank[5][:, :], c1_b[:, :], ALU.add).then_inc(su_dve, 1)
            xT_(2, None)
            xT_(3, None)
            copy_256(WkT, 0, bank[4], 19)
            copy_256(WkT, 1, bank[5], 20)
            dve.wait_ge(su_act, 13)
            minus(V1[1][:, :, :], WvN, V1[0][:, :, :]).then_inc(su_dve, 1)
            dve.wait_ge(su_act, 14)
            nc.vector.tensor_tensor(bvK[64:65, :], bv1_b[64:65, :],
                                    fp(w[0][64:65, :, :, :].rearrange("p a b c -> p (a b c)")[:, 0:D]),
                                    ALU.subtract).then_inc(su_dve, 1)
            dve.wait_ge(su_dve, 8)
            u_(0, None)
            u_(1, None)
            A_lo(A1[1], A1[0], 0, bank[6], 15)
            maxima0(0, None)
            A_lo(A1[1], A1[0], 1, bank[7], 16)
            maxima0(1, None)
            tp("PTa", None, False, flat(PT[1], 0), flat(PT[0], 0))
            dve.wait_ge(su_full, 23)
            nc.vector.tensor_scalar(g1_b[:, :], bank[5][:, :], SCALE, None, ALU.mult).then_inc(su_dve, 1)
            tp("PTb", None, False, flat(PT[1], 1), flat(PT[0], 1))
            dve.wait_ge(su_dve, 18)

            def body(i, par, last, first=False):
                P_inv(i)
                if not first:
                    statistics(2, i - 1, False, 1 - par)
                pj("Pa", i, last, flat(PcT[1], 0), flat(PcT[0], 0))
                if not last:
                    cT_(0, i, 1 - par)
                if not first:
                    statistics(3, i - 1, False, 1 - par)
                pj("Pb", i, last, flat(PcT[1], 1), flat(PcT[0], 1))
                if not last:
                    cT_(1, i, 1 - par)
                if not first:
                    variances(i - 1)
                for r in range(4):
                    if not last:
                        xT_(r, i)
                    x1(r, i, last, par)
                yT_(0, 0, i, last)
                yT_(0, 1, i, last)
                dot(0, i, last, par)
                dot(1, i, last, par)
                if not last:
                    u_(0, i)
                yT_(1, 0, i, last)
                v_(0, i, last)
                g_(0, i, last)
                yT_(1, 1, i, last)
                dot(2, i, last, par)
                dot(3, i, last, par)
                if not last:
                    u_(1, i)
                maxima1(0, i, last)
                w_inv(0, i, last)
                v_(1, i, last)
                w_(0, i)
                g_(1, i, last)
                if not last:
                    maxima0(0, i)
                maxima1(1, i, last)
                s_(0, i, last)
                wa_hi(i, last)
                pj("wa", i, last, flat(wcT[1], 0), flat(wcT[0], 0))
                w_inv(1, i, last)
                w_(1, i)
                if not last:
                    maxima0(1, i)
                    tp("PTa", i, last, flat(PT[1], 0), flat(PT[0], 0))
                x2(0, i, last, par)
                s_(1, i, last)
                pj("wb", i, last, flat(wcT[1], 1), flat(wcT[0], 1))
                x2(1, i, last, par)
                if not last:
                    tp("PTb", i, last, flat(PT[1], 1), flat(PT[0], 1))
                statistics(0, i, last, par)
                x2(2, i, last, par)
                statistics(1, i, last, par)
                x2(3, i, last, par)

            body(0, 0, False, True)
            body(1, 1, False)
            with dve.Fori(1, PAIRS // 2 - 1) as j:
                body(2 * j, 0, False)
                body(2 * j + 1, 1, False)
            body(PAIRS - 2, 0, False)
            body(PAIRS - 1, 1, True)
            statistics(2, PAIRS - 1, True, 1)
            statistics(3, PAIRS - 1, True, 1)
            variances(PAIRS - 1)
            dve.wait_ge(norm_set, PAIRS)
            dve.wait_ge(y_out, 16 * (PAIRS - 1))
            for r in range(3):
                nc.vector.scalar_tensor_tensor(Y[:, r, :], R[1][:, r, :], nmu[:, r:r + 1], gamma_b[:, :],
                                               ALU.add, ALU.mult).then_inc(tail_step, 1)
                dve.wait_ge(tail_step, r + 1)
                nc.vector.scalar_tensor_tensor(Y[:, r, :], Y[:, r, :], rstd[:, r:r + 1], beta_b[:, :],
                                               ALU.mult, ALU.add).then_inc(tail_done, 1)

        @block.gpsimd
        def _(pool):
            nc.gpsimd.memset(ident[:, :], 0.0).then_inc(const_set, 1)
            pool.wait_ge(const_set, 1)
            nc.gpsimd.affine_select(out=ident[:, :], in_=ident[:, :], compare_op=ALU.not_equal, fill=1.0,
                                    base=0, pattern=[[-1, P]], channel_multiplier=1).then_inc(const_set, 1)

            def context(i, par):
                pool.wait_ge(Cs_hi, i + 1)
                nc.gpsimd.tensor_tensor(Cs[par][1][:, :, :], C[:, :, :], fp(Cs[par][0][:, :, :]),
                                        ALU.subtract).then_inc(Cs_set, 1)

            def residual(i, par, first=False):
                pool.wait_ge(tp_full, TP.number("xT3", None if first else i - 1) + 1)
                if not (isinstance(i, int) and i < 2):
                    pool.wait_ge(Y_set, 4 * i - 4)
                for r in range(4):
                    done = nc.gpsimd.tensor_tensor(R[par][:, r, :], X[:, r, :], c1_b[:, :], ALU.add)
                done.then_inc(R_set, 1)

            def scales(i):
                pool.wait_ge(mv_set, i + 1)
                nc.gpsimd.tensor_tensor(rstd[:, :], ve[:, :], half[:, :], ALU.pow).then_inc(norm_step, 1)
                pool.wait_ge(norm_step, i + 1)
                nc.gpsimd.tensor_tensor(nmr[:, :], nmu[:, :], rstd[:, :], ALU.mult).then_inc(norm_set, 1)

            def finish(i):
                for r in range(5):
                    if r < 4:
                        pool.wait_ge(Y_set, 4 * i + (r + 1))
                        nc.gpsimd.tensor_tensor(Y[:, r, :], Y[:, r, :], gamma_b[:, :], ALU.mult
                                                ).then_inc(Y_mul, 1)
                    if r > 0:
                        pool.wait_ge(Y_mul, 4 * i + r)
                        done = nc.gpsimd.tensor_tensor(Y[:, r - 1, :], Y[:, r - 1, :], beta_b[:, :], ALU.add)
                done.then_inc(Y_done, 1)

            def body(i, par, first=False):
                if not first:
                    scales(i - 1)
                context(i + 1, 1 - par)
                residual(i + 1, 1 - par)
                if not first:
                    finish(i - 1)

            context(0, 0)
            pool.wait_ge(su_dve, 11)
            pool.wait_ge(su_full, 18)
            residual(0, 0, True)
            body(0, 0, True)
            body(1, 1)
            with pool.Fori(1, PAIRS // 2 - 1) as j:
                body(2 * j, 0)
                body(2 * j + 1, 1)
            body(PAIRS - 2, 0)
            scales(PAIRS - 2)
            finish(PAIRS - 2)
            scales(PAIRS - 1)
            pool.wait_ge(Y_set, 4 * PAIRS - 3)
            nc.gpsimd.tensor_tensor(Y[:, 3, :], Y[:, 3, :], gamma_b[:, :], ALU.mult).then_inc(Y_mul, 1)
            pool.wait_ge(Y_mul, 4 * PAIRS - 3)
            nc.gpsimd.tensor_tensor(Y[:, 3, :], Y[:, 3, :], beta_b[:, :], ALU.add).then_inc(Y_done, 1)


_INS = ["x", "ctx_512", "L0_xattn_Wq", "L0_xattn_bq", "L0_xattn_Wk", "L0_xattn_Wv", "L0_xattn_bv",
        "L0_xattn_Wo", "L0_xattn_bo", "L1_xattn_Wq", "L1_xattn_Wk", "L1_xattn_bk", "L1_xattn_Wv",
        "L1_xattn_bv", "L1_xattn_gamma", "L1_xattn_beta"]


def kernel(**inputs):
    import numpy as _np
    import concourse.bacc as _bacc
    from concourse import mybir as _mybir
    from concourse.bass_utils import run_bass_kernel_spmd as _run

    nc = _bacc.Bacc("TRN2", target_bir_lowering=False, num_devices=1)
    arrays, args = {}, []
    for name in _INS:
        a = _np.ascontiguousarray(inputs[name])
        arrays[f"in_{name}"] = a
        args.append(nc.dram_tensor(f"in_{name}", a.shape, _mybir.dt.from_np(a.dtype), kind="ExternalInput").ap())
    args.append(nc.dram_tensor("out", (NSEQ, S, D), _mybir.dt.float32, kind="ExternalOutput").ap())
    build(nc, *args)
    r = _run(nc, [arrays], core_ids=[0])
    return r.results[0]["out"]
```
